# Optimizing a Trainium2 kernel written in Bass

```python
import numpy as np
import jax
import jax.numpy as jnp

def _softmax(x, axis=-1):
    return jax.nn.softmax(x, axis=axis)

def _gelu(x):
    return jax.nn.gelu(x, approximate=True)

def _silu(x):
    return jax.nn.silu(x)

def _sigmoid(x):
    return jax.nn.sigmoid(x)

def _layernorm(x, axis=-1, eps=1e-05):
    m = jnp.mean(x, axis=axis, keepdims=True)
    v = jnp.var(x, axis=axis, keepdims=True)
    return (x - m) / jnp.sqrt(v + eps)

def _scatter_add(tgt, idx, src, axis=0):
    return tgt.at[idx].add(src)

def _segment_sum(src, seg, n):
    return jax.ops.segment_sum(src, seg, n)
kernel_name = 'mk_gnn_resnorm_d1_gnn_r8_2c6a2f'

def setup_inputs(seed: int=0):
    np.random.seed(seed)
    _w = jnp.asarray

    def _rec_inputs():
        import jax
        import jax.numpy as jnp
        _gk = jax.random.key(seed)
        x = -0.000202 + 1 * jax.random.normal(jax.random.fold_in(_gk, 1), (6250, 128), jnp.float32)
        _s = jax.random.randint(jax.random.fold_in(_gk, 2), (50000,), 0, 6250, jnp.int32)
        _d = jax.random.randint(jax.random.fold_in(_gk, 3), (50000,), 0, 6250, jnp.int32)
        _loop = jnp.arange(6250, dtype=jnp.int32)
        src = jnp.concatenate([_s, _d, _loop])
        dst = jnp.concatenate([_d, _s, _loop])
        _o = jnp.argsort(dst, stable=True)
        src = src[_o]
        dst = dst[_o]
        edge_attr_128 = -8.16379e-05 + 0.999858 * jax.random.normal(jax.random.fold_in(_gk, 12), (106250, 128), jnp.float32)
        return (x, src, dst, edge_attr_128)
    x, src, dst, edge_attr_128 = _rec_inputs()

    def _L0_gnn_setup():
        import jax, jax.numpy as jnp
        import numpy as np
        N = 6250
        E = 100000
        D = 128

        def _egat_conv(x, e, src, dst, W_ni, W_nj, W_fij, W_node, attn):
            f = (x @ W_ni.T)[src] + (x @ W_nj.T)[dst] + e @ W_fij.T
            f = jax.nn.leaky_relu(f, negative_slope=0.2)
            score = f @ attn
            m = jax.ops.segment_max(score, dst, num_segments=N)
            a = jnp.exp(score - m[dst])
            denom = jax.ops.segment_sum(a, dst, num_segments=N)
            a = a / denom[dst]
            h = x @ W_node.T
            h_out = jax.ops.segment_sum(h[src] * a[:, None], dst, num_segments=N)
            return (h_out, f)
        if __name__ == '__main__':
            out = reference(**setup_inputs())
            print(out.shape, out.dtype)
        key = jax.random.key(seed)
        ks = jax.random.split(key, 14)
        stdv = 1.0 / np.sqrt(D)
        u = lambda k, shape: jax.random.uniform(k, shape, jnp.float32, -stdv, stdv)
        inp = {'node_feats': jax.random.normal(ks[0], (N, D), jnp.float32), 'edge_feats': jax.random.normal(ks[1], (E, D), jnp.float32), 'src': jax.random.randint(ks[2], (E,), 0, N), 'dst': jax.random.randint(ks[3], (E,), 0, N), 'W1_ni': u(ks[4], (D, D)), 'W1_nj': u(ks[5], (D, D)), 'W1_fij': u(ks[6], (D, D)), 'W1_node': u(ks[7], (D, D)), 'attn1': u(ks[8], (D,)), 'W2_ni': u(ks[9], (D, D)), 'W2_nj': u(ks[10], (D, D)), 'W2_fij': u(ks[11], (D, D)), 'W2_node': u(ks[12], (D, D)), 'attn2': u(ks[13], (D,))}
        return inp
    _L0_gnn_all = _L0_gnn_setup()
    _L0_gnn_in = {k: v for k, v in _L0_gnn_all.items() if k in ('W1_ni', 'W1_nj', 'W1_fij', 'W1_node', 'attn1', 'W2_ni', 'W2_nj', 'W2_fij', 'W2_node', 'attn2')}
    del _L0_gnn_all
    return {'x': x, 'src': src, 'dst': dst, 'edge_attr_128': edge_attr_128, 'L0_gnn_W1_ni': _L0_gnn_in['W1_ni'], 'L0_gnn_W1_nj': _L0_gnn_in['W1_nj'], 'L0_gnn_W1_fij': _L0_gnn_in['W1_fij'], 'L0_gnn_W1_node': _L0_gnn_in['W1_node'], 'L0_gnn_attn1': _L0_gnn_in['attn1'], 'L0_gnn_W2_ni': _L0_gnn_in['W2_ni'], 'L0_gnn_W2_nj': _L0_gnn_in['W2_nj'], 'L0_gnn_W2_fij': _L0_gnn_in['W2_fij'], 'L0_gnn_W2_node': _L0_gnn_in['W2_node'], 'L0_gnn_attn2': _L0_gnn_in['attn2']}

def reference(x, src, dst, edge_attr_128, L0_gnn_W1_ni, L0_gnn_W1_nj, L0_gnn_W1_fij, L0_gnn_W1_node, L0_gnn_attn1, L0_gnn_W2_ni, L0_gnn_W2_nj, L0_gnn_W2_fij, L0_gnn_W2_node, L0_gnn_attn2):
    import jax
    import jax.numpy as jnp

    def _L0_gnn_ref(node_feats, edge_feats, src, dst, W1_ni, W1_nj, W1_fij, W1_node, attn1, W2_ni, W2_nj, W2_fij, W2_node, attn2):
        import jax, jax.numpy as jnp
        import numpy as np
        N = 6250
        E = 100000
        D = 128

        def _egat_conv(x, e, src, dst, W_ni, W_nj, W_fij, W_node, attn):
            f = (x @ W_ni.T)[src] + (x @ W_nj.T)[dst] + e @ W_fij.T
            f = jax.nn.leaky_relu(f, negative_slope=0.2)
            score = f @ attn
            m = jax.ops.segment_max(score, dst, num_segments=N)
            a = jnp.exp(score - m[dst])
            denom = jax.ops.segment_sum(a, dst, num_segments=N)
            a = a / denom[dst]
            h = x @ W_node.T
            h_out = jax.ops.segment_sum(h[src] * a[:, None], dst, num_segments=N)
            return (h_out, f)
        if __name__ == '__main__':
            out = reference(**setup_inputs())
            print(out.shape, out.dtype)
        h0, h1 = _egat_conv(node_feats, edge_feats, src, dst, W1_ni, W1_nj, W1_fij, W1_node, attn1)
        h0 = jax.nn.relu(h0) + node_feats
        h1 = jax.nn.relu(h1) + edge_feats
        h0b, _ = _egat_conv(h0, h1, src, dst, W2_ni, W2_nj, W2_fij, W2_node, attn2)
        return h0b + node_feats
    x = _layernorm(x + _L0_gnn_ref(x, edge_attr_128, src, dst, L0_gnn_W1_ni, L0_gnn_W1_nj, L0_gnn_W1_fij, L0_gnn_W1_node, L0_gnn_attn1, L0_gnn_W2_ni, L0_gnn_W2_nj, L0_gnn_W2_fij, L0_gnn_W2_node, L0_gnn_attn2), axis=-1)
    return x

_drawn_inputs = setup_inputs


def setup_inputs(seed=0):
    import zlib

    import numpy as np

    out = dict(_drawn_inputs(seed))
    spreads = {}
    factors = {'edge_attr_128': 3.312,
     'L0_gnn_W1_ni': 7.857,
     'L0_gnn_W1_nj': 8.0,
     'L0_gnn_W1_fij': 8.0,
     'L0_gnn_W1_node': 6.513,
     'L0_gnn_attn1': 8.0,
     'L0_gnn_W2_ni': 3.373,
     'L0_gnn_W2_nj': 7.436,
     'L0_gnn_W2_fij': 3.044}
    for name, (base, spread) in spreads.items():
        noise = np.random.default_rng([zlib.crc32(name.encode()), seed]).standard_normal(out[name].shape)
        drawn = base * np.exp(spread * noise) if base else spread * noise
        out[name] = jnp.asarray(drawn.astype(out[name].dtype))
    for name, factor in factors.items():
        out[name] = (out[name] * factor).astype(out[name].dtype)
    return out
```

```python
import concourse.bass as bass
from concourse import mybir
from contextlib import ExitStack

N, E, D = 6250, 106250, 128
P = 128
TG = 4
GC = 4
TC = TG * GC
W = TG * P
CH = -(-E // (TC * P))
NT = CH * TC
NG = CH * GC
NS = -(-(N + P) // W)
NP = NS * W
XB = 3
BIG = 1e38
SLOPE = 0.2
EPS = 1e-5
SORTED = "dst lies in [0, N], its padding at N"


class Layer:

    def __init__(self, sem, n, edges_in, proj_dst, table, g2_out):
        self.n = n
        self.edges_in, self.proj_dst, self.table, self.g2_out = edges_in, proj_dst, table, g2_out
        self.loaded = [sem(f"loaded{n}_{g}") for g in range(GC)]
        self.gathered = [[sem(f"gathered{n}_{b}_{g}") for g in range(GC)] for b in range(XB)]
        self.idx_ready = sem(f"idx_ready{n}")
        self.xt_made = sem(f"xt_made{n}")
        self.xt_copied = sem(f"xt_copied{n}")
        self.onehot_made = sem(f"onehot_made{n}")
        self.z_made = sem(f"z_made{n}")
        self.z_copied = sem(f"z_copied{n}")
        self.z_used = sem(f"z_used{n}")
        self.f_made = sem(f"f_made{n}")
        self.score_made = sem(f"score_made{n}")
        self.score_copied = sem(f"score_copied{n}")
        self.g2_made = sem(f"g2_made{n}")
        self.g2_copied = sem(f"g2_copied{n}")
        self.g2_stored = [sem(f"g2_stored{n}_{g}") for g in range(GC)]
        self.soft_pe = sem(f"soft_pe{n}")
        self.soft_dve = sem(f"soft_dve{n}")
        self.soft_act = sem(f"soft_act{n}")
        self.a_made = sem(f"a_made{n}")
        self.num_made = sem(f"num_made{n}")
        self.num_added = sem(f"num_added{n}")
        self.dve_step = sem(f"dve_step{n}")


class Steps:

    def __init__(self, eng, sem):
        self.eng, self.sem, self.base, self.k = eng, sem, 0, 0

    def __call__(self, ins):
        self.k += 1
        ins.then_inc(self.sem, 1)
        self.eng.wait_ge(self.sem, self.base + self.k)


def above(eng, sem, value):
    if not isinstance(value, int) or value > 0:
        eng.wait_ge(sem, value)


def program(nc, eT, xT, xrows, idxT, dstT, dstR, dst8, ends, w_fij1, w_ni1, w_nj1, w_node1, attn1,
            w_fij2, w_ni2, w_nj2, w_node2, attn2, out):
    f32, bf16, i32 = mybir.dt.float32, mybir.dt.bfloat16, mybir.dt.int32
    ALU, ACT = mybir.AluOpType, mybir.ActivationFunctionType
    PE_, DVE_, SP_ = mybir.EngineType.PE, mybir.EngineType.DVE, mybir.EngineType.SP

    proj1 = nc.dram_tensor("proj1", [NP, D], f32, kind="Internal").ap()
    proj2 = nc.dram_tensor("proj2", [NP, D], f32, kind="Internal").ap()
    h0rows = nc.dram_tensor("h0rows", [NP, D], f32, kind="Internal").ap()
    g2T = nc.dram_tensor("g2T", [NG, P, W], f32, kind="Internal").ap()
    relrow = nc.dram_tensor("relrow", [NG, W], bf16, kind="Internal").ap()

    ctx = ExitStack()
    with ctx:
        def sb(name, shape, dt=f32):
            return ctx.enter_context(nc.sbuf_tensor(name, shape, dt))

        def pb(name):
            return ctx.enter_context(nc.psum_tensor(name, [P, W], f32))

        def sem(name):
            return ctx.enter_context(nc.semaphore(name))

        ident = sb("ident", [P, P])
        iota_row = sb("iota_row", [P, P])
        iota_col = sb("iota_col", [P, 1])
        ones = sb("ones", [P, P])
        wts = sb("wts", [P, 8, P])
        attn = sb("attn", [P, 2])
        FIJ, NI, NJ, NODE = 0, 1, 2, 3

        idx_all = sb("idx_all", [P, NT], i32)
        dst_rows = sb("dst_rows", [TC, CH, P], i32)
        rel_col = sb("rel_col", [P, NT])
        base_all = sb("base_all", [P, NT], i32)
        base_row = sb("base_row", [1, NT], i32)
        last_row = sb("last_row", [1, NT], i32)
        cont = sb("cont", [1, NT + 1])
        whole = sb("whole", [1, NT + 1])
        keepA = sb("keepA", [1, NT + 1])
        keepE = sb("keepE", [1, NT + 1])
        penC = sb("penC", [1, NT + 1])
        penA = sb("penA", [1, NT + 1])
        penE = sb("penE", [1, NT + 1])
        dst8_t = sb("dst8_t", [NT // 8, 8, P], i32)
        rel8 = sb("rel8", [NT // 8, 8, P], bf16)

        edge_in = [sb(f"edge_in{g}", [P, W]) for g in range(GC)]
        window = [sb(f"window{g}", [P, TG, P]) for g in range(GC)]
        rel_bc = [sb(f"rel_bc{g}", [P, W], bf16) for g in range(GC)]
        xsrc = [sb(f"xsrc{b}", [P, TC, P]) for b in range(XB)]
        idx_slot = [sb(f"idx_slot{b}", [P, TC], i32) for b in range(XB)]
        xsT = [sb(f"xsT{s}", [P, W]) for s in range(2)]
        onehot = [sb(f"onehot{s}", [P, W]) for s in range(2)]
        zc = [sb(f"zc{s}", [P, W]) for s in range(2)]
        zs = [sb(f"zs{s}", [P, W]) for s in range(2)]
        fT = [sb(f"fT{s}", [P, W]) for s in range(2)]
        g2s = [sb(f"g2s{g}", [P, W]) for g in range(GC)]
        amat = [sb(f"amat{s}", [P, TG, P]) for s in range(2)]
        numT = sb("numT", [P, NP])

        score_sb = sb("score_sb", [P, TC])
        keep = sb("keep", [TC, P + 1])
        pen = sb("pen", [TC, P + 1])
        isF = sb("isF", [TC, P])
        isL = sb("isL", [TC, P])
        penF = sb("penF", [TC, P])
        penL = sb("penL", [TC, P])
        scanF = sb("scanF", [TC, P])
        scanB = sb("scanB", [TC, P])
        seg = sb("seg", [TC, P])
        aexp = sb("aexp", [TC, P])
        wrow = sb("wrow", [TC, P])
        cd = sb("cd", [TC, 2])
        rowC = sb("rowC", [1, TC + 1])
        rowD = sb("rowD", [1, TC])
        sumC = sb("sumC", [1, TC + 1])
        sumD = sb("sumD", [1, TC])
        u1 = sb("u1", [1, TC])
        u2 = sb("u2", [1, TC])
        u3 = sb("u3", [1, TC])
        ecar = sb("ecar", [1, 2])
        cfac = sb("cfac", [1, 1])
        wcol = sb("wcol", [P, TC + 1])
        relc = sb("relc", [P, TC])

        slab = [sb(f"slab{s}", [P, W]) for s in range(2)]
        natA = [sb(f"natA{s}", [P, TG, P]) for s in range(2)]
        natB = [sb(f"natB{s}", [P, TG, P]) for s in range(2)]
        stats = sb("stats", [P, TG, 6])
        mv = sb("mv", [P, TG, 2])
        std = sb("std", [P, TG])
        rstd = sb("rstd", [P, TG])

        bXT, bG2, bSC, bSM = pb("bXT"), pb("bG2"), pb("bSC"), pb("bSM")
        bZ = [pb("bZ0"), pb("bZ1")]
        bAG = [pb("bAG0"), pb("bAG1")]
        ROWS = bSM[0:TC, 0:P]
        END_F, END_B = bSM[0:1, 128:128 + TC], bSM[0:1, 144:144 + TC]
        CD = bSM[0:TC, 160:162]
        SEND_F, SEND_B = bSM[0:1, 192:192 + TC], bSM[0:1, 208:208 + TC]
        SCD = bSM[0:TC, 224:226]
        WCOL = bSM[:, 256:256 + TC + 1]

        pe_passed, dve_passed, pool_passed = sem("pe_passed"), sem("dve_passed"), sem("pool_passed")
        const_in = sem("const_in")
        idx_in = sem("idx_in")
        graph_in = sem("graph_in")
        rel8_in = sem("rel8_in")
        const_made = sem("const_made")
        iota_made = sem("iota_made")
        rel8_made = sem("rel8_made")
        rel_stored = sem("rel_stored")
        rel_made = sem("rel_made")
        dve_pro = sem("dve_pro")
        L1 = Layer(sem, 1, eT, proj1, xrows, g2T)
        L2 = Layer(sem, 2, g2T, proj2, h0rows, None)
        p_in = [sem("p_in0"), sem("p_in1")]
        p_made = sem("p_made")
        p_copied = sem("p_copied")
        p_stored = [sem("p_stored0"), sem("p_stored1")]
        m_in = [sem("m_in0"), sem("m_in1")]
        m_ht = sem("m_ht")
        m_h0 = sem("m_h0")
        m_zero = sem("m_zero")
        m_proj = sem("m_proj")
        m_rows = sem("m_rows")
        m_proj_copied = sem("m_proj_copied")
        m_rows_copied = sem("m_rows_copied")
        m_proj_stored = [sem("m_proj_stored0"), sem("m_proj_stored1")]
        m_rows_stored = [sem("m_rows_stored0"), sem("m_rows_stored1")]
        e_in = [sem("e_in0"), sem("e_in1")]
        e_ht = sem("e_ht")
        e_y = sem("e_y")
        e_rows = sem("e_rows")
        e_var = sem("e_var")
        e_std = sem("e_std")
        e_out = sem("e_out")
        e_dve = sem("e_dve")
        e_stored = [sem("e_stored0"), sem("e_stored1")]

        block = ctx.enter_context(nc.Block())
        consts = [w_fij1, w_ni1, w_nj1, w_node1, w_fij2, w_ni2, w_nj2, w_node2]
        rows4 = lambda t, m: t[bass.ds(m * W, W), :].rearrange("(b p) d -> p b d", p=P)

        def slabs(eng, body):
            body(0, 0, 0)
            body(1, 1, 0)
            turns = NS // 2 - 1
            with eng.Fori(0, turns) as j:
                body(j * 2 + 2, 0, j + 1)
                body(j * 2 + 3, 1, j + 1)
            for m in range(2 + 2 * turns, NS):
                body(m, m % 2, m // 2)

        @block.sync
        def _(sp):
            sp.dma_start(dst8_t[:, :, :], dst8).then_inc(rel8_in, 16)
            sp.dma_start(base_all[:, :], ends[0:1, :].partition_broadcast(P)).then_inc(graph_in, 16)
            sp.dma_start(rel_col[:, :].bitcast(i32), dstT).then_inc(graph_in, 16)
            sp.dma_start(base_row[:, :], ends[0:1, :]).then_inc(graph_in, 16)
            sp.dma_start(last_row[:, :], ends[1:2, :]).then_inc(graph_in, 16)
            sp.dma_start(dst_rows[:, :, :], dstR).then_inc(graph_in, 16)

            def slab_in(arrived, used):
                def body(m, s, r):
                    above(sp, used, m - 1)
                    sp.dma_start(slab[s][:, :], xT[:, bass.ds(m * W, W)]).then_inc(arrived[s], 16)
                return body

            slab_p = slab_in(p_in, p_made)
            slabs(sp, slab_p)

            sp.wait_ge(rel8_made, 1)
            sp.dma_start(relrow.rearrange("(p a) w -> p (a w)", a=2),
                         rel8[:, :, :].rearrange("p a e -> p (a e)")).then_inc(rel_stored, 16)
            sp.wait_ge(rel_stored, 16)

            def load_layer(L):
                def chunk(c):
                    _, first = nc.values_load_multi_w_load_instructions(
                        base_row[0:1, bass.ds(c * TC, TC)], engines=(SP_,), min_val=0, max_val=N,
                        skip_runtime_bounds_check_because=SORTED)
                    for g in range(GC):
                        n = c * GC + g
                        above(sp, L.z_made, n - (GC - 1))
                        above(sp, L.z_used, n - (GC - 1))
                        sp.dma_start(edge_in[g][:, :], L.edges_in[bass.ds(n, 1), :, :].rearrange(
                            "o p w -> (o p) w")).then_inc(L.loaded[g], 16)
                        sp.dma_start(rel_bc[g][:, :], relrow[bass.ds(n, 1), :].partition_broadcast(P)
                                     ).then_inc(L.loaded[g], 16)
                        for i in range(TG):
                            sp.dma_start(window[g][:, i, :], L.proj_dst[bass.ds(first[g * TG + i], P), :]
                                         ).then_inc(L.loaded[g], 16)
                        if L.g2_out is not None and not (isinstance(c, int) and c == 0):
                            store_g2(L, c - 1, g)
                return chunk

            def store_g2(L, c, g):
                n = c * GC + g
                sp.wait_ge(L.g2_copied, n + 1)
                sp.dma_start(L.g2_out[bass.ds(n, 1), :, :].rearrange("o p w -> (o p) w"), g2s[g][:, :]
                             ).then_inc(L.g2_stored[g], 16)

            def layer(L):
                chunk = load_layer(L)
                chunk(0)
                with sp.Fori(1, CH) as c:
                    chunk(c)
                if L.g2_out is not None:
                    for g in range(GC):
                        store_g2(L, CH - 1, g)
                    for g in range(GC):
                        sp.wait_ge(L.g2_stored[g], 16 * CH)

            for s in range(2):
                sp.wait_ge(p_stored[s], 16 * ((NS + 1 - s) // 2))
            sp.wait_ge(graph_in, 16 * 5)
            layer(L1)

            slab_m = slab_in(m_in, m_h0)

            def middle(m, s, r):
                slab_m(m, s, r)
                if not isinstance(m, int) or m >= 1:
                    rows_out(m - 1, 1 - s)

            def rows_out(m, s):
                sp.wait_ge(m_rows_copied, m + 1)
                sp.dma_start(rows4(h0rows, m), natB[s][:, :, :]).then_inc(m_rows_stored[s], 16)

            slabs(sp, middle)
            rows_out(NS - 1, (NS - 1) % 2)
            for s in range(2):
                sp.wait_ge(m_rows_stored[s], 16 * ((NS + 1 - s) // 2))
                sp.wait_ge(m_proj_stored[s], 16 * ((NS + 1 - s) // 2))
            layer(L2)

            slab_e = slab_in(e_in, e_y)

            def end(m, s, r):
                slab_e(m, s, r)
                if not isinstance(m, int) or m >= 1:
                    y_out(m - 1, 1 - s)

            def y_out(m, s):
                sp.wait_ge(e_out, m + 1)
                sp.dma_start(rows4(out, m), natA[s][:, :, :]).then_inc(e_stored[s], 16)

            slabs(sp, end)
            m, s = NS - 1, (NS - 1) % 2
            sp.wait_ge(e_out, m + 1)
            sp.dma_start(out[m * W:N, :], natA[s][0:N - m * W, 0, :]).then_inc(e_stored[s], 16)
            for s in range(2):
                sp.wait_ge(e_stored[s], 16 * ((NS + 1 - s) // 2))

        @block.gpsimd
        def _(pool):
            pool.dma_start(idx_all[:, :], idxT).then_inc(idx_in, 16)
            nc.gpsimd.iota(iota_row[:, :], [[1, P]], base=0, channel_multiplier=0,
                           allow_small_or_imprecise_dtypes=True).then_inc(iota_made, 1)
            nc.gpsimd.iota(iota_col[:, :], [[0, 1]], base=0, channel_multiplier=1,
                           allow_small_or_imprecise_dtypes=True).then_inc(iota_made, 1)
            nc.gpsimd.memset(ones[:, :], 1.0).then_inc(iota_made, 1)
            pool.wait_ge(iota_made, 3)
            nc.gpsimd.affine_select(out=ident[:, :], in_=ones[:, :], compare_op=ALU.is_equal, fill=0.0,
                                    base=0, pattern=[[-1, P]], channel_multiplier=1).then_inc(const_made, 1)
            pool.wait_ge(idx_in, 16)

            def layer(L):
                def chunk(c, b, again):
                    if again:
                        pool.wait_ge(L.num_made, (c - XB) * GC + 1)
                    nc.gpsimd.tensor_copy(idx_slot[b][:, :], idx_all[:, bass.ds(c * TC, TC)]
                                          ).then_inc(L.idx_ready, 1)
                    pool.wait_ge(L.idx_ready, c + 1)
                    pool.sem_inc(pool_passed, 1)
                    for g in range(GC):
                        if again:
                            pool.wait_ge(L.num_made, (c - XB) * GC + g + 1)
                            pool.sem_inc(pool_passed, 1)
                        for i in range(g * TG, g * TG + TG):
                            pool.indirect_dma_start(
                                xsrc[b][:, i, :], None, L.table,
                                bass.IndirectOffsetOnAxis(ap=idx_slot[b][:, i:i + 1], axis=0)
                            ).then_inc(L.gathered[b][g], 16)

                for c in range(XB):
                    chunk(c, c, False)
                turns = (CH - XB) // XB
                with pool.Fori(0, turns) as j:
                    for b in range(XB):
                        chunk(j * XB + (XB + b), b, True)
                for c in range(XB + turns * XB, CH):
                    chunk(c, c % XB, True)

            layer(L1)
            for s in range(2):
                pool.wait_ge(m_rows_stored[s], 16 * ((NS + 1 - s) // 2))
            layer(L2)

        @block.scalar
        def _(act):
            for k, w in enumerate(consts):
                act.dma_start(wts[:, k, :], w).then_inc(const_in, 16)
            act.dma_start(attn[:, 0:1], attn1).then_inc(const_in, 16)
            act.dma_start(attn[:, 1:2], attn2).then_inc(const_in, 16)

            def project(m, s, r):
                act.wait_ge(p_made, m + 1)
                above(act, p_stored[s], r * 16)
                nc.scalar.copy(natA[s][:, :, :].rearrange("p b d -> p (b d)"), bAG[s][:, :]).then_inc(p_copied, 1)
                act.wait_ge(p_copied, m + 1)
                act.dma_start(rows4(proj1, m), natA[s][:, :, :]).then_inc(p_stored[s], 16)

            slabs(act, project)

            def layer(L):
                def slot(c, g, front, soft):
                    n, s = c * GC + g, g % 2
                    if front:
                        act.wait_ge(L.xt_made, n + 1)
                        above(act, L.z_made, n - 1)
                        nc.scalar.copy(xsT[s][:, :], bXT[:, :]).then_inc(L.xt_copied, 1)
                    if soft and g == 2:
                        act.wait_ge(L.soft_dve, (c - 1) * 6 + 3)
                        nc.scalar.activation(aexp[:, :], seg[:, :], ACT.Exp)
                        nc.scalar.activation(ecar[0:1, 1:2], ecar[0:1, 0:1], ACT.Exp).then_inc(L.soft_act, 1)
                    if front and L.g2_out is not None:
                        act.wait_ge(L.z_made, n + 1)
                        above(act, L.z_used, n - 1)
                        nc.scalar.copy(zc[s][:, :], bZ[s][:, :]).then_inc(L.z_copied, 1)
                    if g == 0 and soft:
                        act.wait_ge(L.score_made, c * GC)
                        nc.scalar.copy(score_sb[:, :], bSC[:, 0:TC]).then_inc(L.score_copied, 1)
                    if L.g2_out is not None and not (isinstance(c, int) and (n == 0 or n > NG)):
                        q = (g - 1) % GC
                        act.wait_ge(L.g2_made, n)
                        above(act, L.g2_stored[q], (c - (1 if g == 0 else 0)) * 16)
                        nc.scalar.copy(g2s[q][:, :], bG2[:, :]).then_inc(L.g2_copied, 1)

                def turn(c, front, soft):
                    for g in range(GC):
                        slot(c, g, front, soft)

                turn(0, True, False)
                turn(1, True, True)
                with act.Fori(2, CH) as c:
                    turn(c, True, True)
                turn(CH, False, True)

            layer(L1)

            def middle(m, s, r):
                act.wait_ge(m_proj, m + 1)
                above(act, m_proj_stored[s], r * 16)
                nc.scalar.copy(natA[s][:, :, :].rearrange("p b d -> p (b d)"), bAG[s][:, :]
                               ).then_inc(m_proj_copied, 1)
                act.wait_ge(m_proj_copied, m + 1)
                act.dma_start(rows4(proj2, m), natA[s][:, :, :]).then_inc(m_proj_stored[s], 16)

            slabs(act, middle)
            layer(L2)

            def end(m, s, r):
                act.wait_ge(e_var, m + 1)
                nc.scalar.activation(std[:, :], std[:, :], ACT.Sqrt).then_inc(e_std, 1)

            slabs(act, end)

        @block.tensor
        def _(pe):
            mm, tp = nc.tensor.matmul, nc.tensor.transpose
            pe.wait_ge(const_made, 1)
            pe.wait_ge(const_in, 16 * 10)

            def project(m, s, r):
                pe.wait_ge(p_in[s], (r + 1) * 16)
                above(pe, p_copied, m - 1)
                for b in range(TG):
                    last = mm(bAG[s][:, b * P:b * P + P], slab[s][:, b * P:b * P + P], wts[:, NJ, :],
                              start=True, stop=True)
                last.then_inc(p_made, 1)

            slabs(pe, project)

            def layer(L):
                fij, ni = wts[:, FIJ, :], wts[:, (L.n - 1) * 4 + NI, :]
                at = attn[:, L.n - 1:L.n]
                one = L.g2_out is not None

                def front(c, g, b, rounds):
                    n, s = c * GC + g, g % 2
                    pe.wait_ge(L.gathered[b][g], (rounds + 1) * 16 * TG)
                    above(pe, L.xt_copied, n)
                    for i in range(TG):
                        last = tp(bXT[:, i * P:i * P + P], xsrc[b][:, g * TG + i, :], ident[:, :])
                    last.then_inc(L.xt_made, 1)
                    above(pe, L.z_copied if one else L.z_used, n - 1)
                    if one:
                        pe.wait_ge(L.loaded[g], (c + 1) * 96)
                        mm(bZ[s][:, :], fij, edge_in[g][:, :], start=True, stop=False)
                    pe.wait_ge(L.xt_copied, n + 1)
                    mm(bZ[s][:, :], ni, xsT[s][:, :], start=not one, stop=False)
                    if not one:
                        pe.wait_ge(L.loaded[g], (c + 1) * 96)
                    pe.wait_ge(L.onehot_made, n + 1)
                    for i in range(TG):
                        last = mm(bZ[s][:, i * P:i * P + P], window[g][:, i, :], onehot[s][:, i * P:i * P + P],
                                  start=False, stop=i == TG - 1)
                    last.then_inc(L.z_made, 1)

                def scores(c, g, after):
                    n, s = c * GC + g, g % 2
                    pe.wait_ge(L.f_made, n + 1)
                    if g == 0:
                        above(pe, L.score_copied, c)
                    for i in range(TG):
                        t = g * TG + i
                        last = mm(bSC[:, t:t + 1], fT[s][:, i * P:i * P + P], at, start=True, stop=True)
                    last.then_inc(L.score_made, 1)
                    if one:
                        pe.wait_ge(L.z_used, n + 1)
                        above(pe, L.g2_copied, n)
                        mm(bG2[:, :], wts[:, 4 + FIJ, :], zs[s][:, :], start=True, stop=True).then_inc(L.g2_made, 1)

                def partial(k, g, b):
                    n, s = k * GC + g, g % 2
                    pe.wait_ge(L.a_made, n + 1)
                    above(pe, L.num_added, n - 1)
                    for i in range(TG):
                        last = mm(bAG[s][:, i * P:i * P + P], xsrc[b][:, g * TG + i, :], amat[s][:, i, :],
                                  start=True, stop=True)
                    last.then_inc(L.num_made, 1)

                def to_rows(k):
                    pe.wait_ge(L.score_copied, k + 1)
                    above(pe, L.soft_dve, k * 6)
                    tp(ROWS, score_sb[:, :], ident[:, :]).then_inc(L.soft_pe, 1)

                def ends_to_row(k, step, f, b):
                    pe.wait_ge(L.soft_dve, k * 6 + step)
                    pe.sem_inc(pe_passed, 1)
                    tp(f, scanF[:, P - 1:P], ident[0:TC, 0:TC])
                    tp(b, scanB[:, 0:1], ident[0:TC, 0:TC]).then_inc(L.soft_pe, 1)

                def row_to_cols(k, step, cols, c_row, d_row):
                    pe.wait_ge(L.soft_dve, k * 6 + step)
                    pe.sem_inc(pe_passed, 1)
                    tp(cols[:, 0:1], c_row[0:1, 0:TC], ident[0:1, 0:1])
                    tp(cols[:, 1:2], d_row[0:1, 0:TC], ident[0:1, 0:1]).then_inc(L.soft_pe, 1)

                def weights_to_cols(k):
                    pe.wait_ge(L.soft_dve, k * 6 + 6)
                    pe.sem_inc(pe_passed, 1)
                    tp(WCOL[:, 0:TC], wrow[:, :], ident[0:TC, 0:TC])
                    mm(WCOL[:, TC:TC + 1], ones[0:1, :], cfac[0:1, 0:1], start=True, stop=True
                       ).then_inc(L.soft_pe, 1)

                def turn(c, b, rounds, has_front, soft, agg):
                    for g in range(GC):
                        if has_front:
                            front(c, g, b, rounds)
                        if soft and g == 1:
                            ends_to_row(c - 1, 1, END_F, END_B)
                        if soft and g == 3:
                            row_to_cols(c - 1, 5, SCD, sumC, sumD)
                        if g == 0:
                            if soft:
                                scores(c - 1, GC - 1, None)
                        elif has_front:
                            scores(c, g - 1, None)
                        if agg:
                            partial(c - 2, g, (b - 2) % XB)
                        if soft and g == 0:
                            to_rows(c - 1)
                        if soft and g == 1:
                            row_to_cols(c - 1, 2, CD, rowC, rowD)
                        if soft and g == 2:
                            ends_to_row(c - 1, 4, SEND_F, SEND_B)
                        if soft and g == 3:
                            weights_to_cols(c - 1)

                for c in range(XB):
                    turn(c, c, 0, True, c >= 1, c >= 2)
                turns = (CH - XB) // XB
                with pe.Fori(0, turns) as j:
                    for b in range(XB):
                        turn(j * XB + (XB + b), b, j + 1, True, True, True)
                for c in range(XB + turns * XB, CH + 2):
                    turn(c, c % XB, c // XB, c < CH, c <= CH, True)

            layer(L1)

            def node_sum(made, used, node, m, s):
                above(pe, used, m - 1)
                mm(bZ[s][:, :], node, numT[:, bass.ds(m * W, W)], start=True, stop=True).then_inc(made, 1)

            def middle_rest(m, s):
                pe.wait_ge(m_h0, m + 1)
                above(pe, m_proj_copied, m - 1)
                for b in range(TG):
                    last = mm(bAG[s][:, b * P:b * P + P], zs[s][:, b * P:b * P + P], wts[:, 4 + NJ, :],
                              start=True, stop=True)
                last.then_inc(m_proj, 1)
                bank = (bXT, bG2)[s]
                above(pe, m_rows_copied, m - 1)
                for b in range(TG):
                    last = tp(bank[:, b * P:b * P + P], zs[s][:, b * P:b * P + P], ident[:, :])
                last.then_inc(m_rows, 1)

            def middle(m, s, r):
                node_sum(m_ht, m_h0, wts[:, NODE, :], m, s)
                if not isinstance(m, int) or m >= 1:
                    middle_rest(m - 1, 1 - s)

            pe.wait_ge(L1.num_added, NG)
            slabs(pe, middle)
            middle_rest(NS - 1, (NS - 1) % 2)

            layer(L2)

            def end_rest(m, s):
                pe.wait_ge(e_y, m + 1)
                above(pe, e_out, m - 1)
                for b in range(TG):
                    last = tp(bAG[s][:, b * P:b * P + P], zs[s][:, b * P:b * P + P], ident[:, :])
                last.then_inc(e_rows, 1)

            def end(m, s, r):
                node_sum(e_ht, e_y, wts[:, 4 + NODE, :], m, s)
                if not isinstance(m, int) or m >= 1:
                    end_rest(m - 1, 1 - s)

            pe.wait_ge(L2.num_added, NG)
            slabs(pe, end)
            end_rest(NS - 1, (NS - 1) % 2)

        @block.vector
        def _(dve):
            v = nc.vector
            step = Steps(dve, dve_pro)
            dve.wait_ge(rel8_in, 16)
            v.tensor_tensor(rel8[:, :, :], dst8_t[:, :, :], dst8_t[:, :, 0:1].broadcast_to((NT // 8, 8, P)),
                            ALU.subtract).then_inc(rel8_made, 1)
            v.memset(numT[:, :], 0.0)
            v.memset(keep[:, :], 0.0)
            step(v.memset(pen[:, :], 0.0))
            dve.wait_ge(graph_in, 16 * 5)
            v.tensor_tensor(rel_col[:, :], rel_col[:, :].bitcast(i32), base_all[:, :], ALU.subtract)
            v.memset(cont[:, :], 0.0)
            v.memset(whole[:, :], 0.0)
            v.memset(keepA[:, :], 0.0)
            step(v.memset(keepE[:, :], 0.0))
            v.tensor_tensor(cont[0:1, 1:NT], base_row[0:1, 1:NT], last_row[0:1, 0:NT - 1], ALU.is_equal)
            step(v.tensor_tensor(whole[0:1, 0:NT], base_row[0:1, :], last_row[0:1, :], ALU.is_equal))
            v.tensor_tensor(keepA[0:1, 1:NT + 1], cont[0:1, 1:NT + 1], whole[0:1, 0:NT], ALU.mult)
            step(v.tensor_tensor(keepE[0:1, :], cont[0:1, :], whole[0:1, :], ALU.mult))
            v.tensor_scalar(penC[0:1, :], cont[0:1, :], BIG, -BIG, ALU.mult, ALU.add)
            v.tensor_scalar(penA[0:1, :], keepA[0:1, :], BIG, -BIG, ALU.mult, ALU.add)
            step(v.tensor_scalar(penE[0:1, :], keepE[0:1, :], BIG, -BIG, ALU.mult, ALU.add))
            dve.wait_ge(iota_made, 3)

            def layer(L):
                one = L.g2_out is not None
                step = Steps(dve, L.dve_step)

                v.memset(rowC[:, :], -BIG)
                v.memset(sumC[:, :], 0.0)
                v.memset(sumD[:, :], 0.0)
                step(v.memset(rowD[:, :], -BIG))

                def masks(k):
                    d = dst_rows[:, k, :]
                    v.tensor_tensor(keep[:, 1:P], d[:, 1:P], d[:, 0:P - 1], ALU.is_equal)
                    v.tensor_tensor(isF[:, :], d, d[:, 0:1].broadcast_to((TC, P)), ALU.is_equal)
                    step(v.tensor_tensor(isL[:, :], d, d[:, P - 1:P].broadcast_to((TC, P)), ALU.is_equal))
                    v.tensor_scalar(pen[:, 1:P], keep[:, 1:P], BIG, -BIG, ALU.mult, ALU.add)
                    v.tensor_scalar(penF[:, :], isF[:, :], BIG, -BIG, ALU.mult, ALU.add)
                    step(v.tensor_scalar(penL[:, :], isL[:, :], BIG, -BIG, ALU.mult, ALU.add))

                def row_maxima(k):
                    dve.wait_ge(L.soft_pe, k * 6 + 1)
                    v.tensor_tensor_scan(scanF[:, :], pen[:, 0:P], ROWS, -BIG, ALU.add, ALU.max)
                    step(v.tensor_tensor_scan(scanB[:, ::-1], pen[:, P:0:-1], ROWS[:, ::-1], -BIG, ALU.add, ALU.max))
                    v.tensor_tensor(seg[:, :], scanF[:, :], scanB[:, :], ALU.max).then_inc(L.soft_dve, 1)

                def chain(k, at, ends_f, ends_b, from_before, row, back, pa, pe_, pc, op0, op1, last):
                    dve.wait_ge(L.soft_pe, k * 6 + at)
                    v.tensor_tensor(u1[0:1, :], ends_f, pc[0:1, bass.ds(k * TC + 1, TC)], op0)
                    if from_before is None:
                        v.tensor_copy(row[0:1, 0:1], row[0:1, TC:TC + 1])
                    else:
                        v.tensor_tensor(row[0:1, 0:1], row[0:1, TC:TC + 1], from_before, ALU.mult)
                    v.tensor_copy(u3[0:1, 0:TC - 1], pe_[0:1, bass.ds(k * TC + 1, TC - 1)])
                    step(v.tensor_tensor(u2[0:1, 0:TC - 1], ends_b[0:1, 1:TC], pc[0:1, bass.ds(k * TC + 1, TC - 1)],
                                         op0))
                    v.tensor_tensor_scan(row[0:1, 1:TC + 1], pa[0:1, bass.ds(k * TC + 1, TC)], u1[0:1, :],
                                         row[0:1, 0:1], op0, op1)
                    v.tensor_tensor_scan(back[0:1, TC - 2::-1], u3[0:1, TC - 2::-1],
                                         u2[0:1, TC - 2::-1], last, op0, op1).then_inc(L.soft_dve, 1)

                def subtract_maxima(k):
                    dve.wait_ge(L.soft_pe, k * 6 + 3)
                    dve.wait_ge(L.soft_dve, k * 6 + 2)
                    step(v.tensor_copy(cd[:, :], CD))
                    step(v.scalar_tensor_tensor(seg[:, :], penF[:, :], cd[:, 0:1], seg[:, :], ALU.add, ALU.max))
                    step(v.scalar_tensor_tensor(seg[:, :], penL[:, :], cd[:, 1:2], seg[:, :], ALU.add, ALU.max))
                    step(v.tensor_tensor(ecar[0:1, 0:1], rowC[0:1, 0:1], seg[0:1, 0:1], ALU.subtract))
                    v.tensor_tensor(seg[:, :], ROWS, seg[:, :], ALU.subtract).then_inc(L.soft_dve, 1)

                def row_sums(k):
                    dve.wait_ge(L.soft_act, k + 1)
                    v.tensor_tensor_scan(scanF[:, :], keep[:, 0:P], aexp[:, :], 0.0, ALU.mult, ALU.add)
                    step(v.tensor_tensor_scan(scanB[:, ::-1], keep[:, P:0:-1], aexp[:, ::-1], 0.0, ALU.mult, ALU.add))
                    step(v.tensor_tensor(seg[:, :], scanF[:, :], aexp[:, :], ALU.subtract))
                    v.tensor_tensor(seg[:, :], seg[:, :], scanB[:, :], ALU.add).then_inc(L.soft_dve, 1)

                def normalise(k):
                    dve.wait_ge(L.soft_pe, k * 6 + 5)
                    dve.wait_ge(L.soft_dve, k * 6 + 5)
                    step(v.tensor_copy(cd[:, :], SCD))
                    step(v.scalar_tensor_tensor(seg[:, :], isF[:, :], cd[:, 0:1], seg[:, :], ALU.mult, ALU.add))
                    step(v.scalar_tensor_tensor(seg[:, :], isL[:, :], cd[:, 1:2], seg[:, :], ALU.mult, ALU.add))
                    step(v.reciprocal(seg[:, :], seg[:, :]))
                    v.tensor_tensor(cfac[0:1, 0:1], sumC[0:1, 0:1], seg[0:1, 0:1], ALU.mult)
                    v.tensor_tensor(wrow[:, :], aexp[:, :], seg[:, :], ALU.mult).then_inc(L.soft_dve, 1)

                def weight_cols(k, base):
                    dve.wait_ge(L.soft_pe, k * 6 + 6)
                    v.tensor_copy(relc[:, :], rel_col[:, bass.ds(k * TC, TC)])
                    step(v.tensor_copy(wcol[:, :], WCOL))
                    col = numT[:, bass.ds(base, 1)]
                    step(v.tensor_scalar(col, col, wcol[:, TC:TC + 1], None, ALU.mult))

                def weighted_onehot(k, g):
                    n, s = k * GC + g, g % 2
                    above(dve, L.num_made, n - 1)
                    for i in range(TG):
                        t = g * TG + i
                        last = v.tensor_scalar(amat[s][:, i, :], iota_row[:, :], relc[:, t:t + 1], wcol[:, t:t + 1],
                                               ALU.is_equal, ALU.mult)
                    last.then_inc(L.a_made, 1)

                def add_sums(n, g, bases):
                    dve.wait_ge(L.num_made, n + 1)
                    for i in range(TG):
                        win = numT[:, bass.ds(bases[i], P)]
                        ins = v.tensor_tensor(win, win, bAG[g % 2][:, i * P:i * P + P], ALU.add)
                        if i < TG - 1:
                            step(ins)
                        else:
                            ins.then_inc(L.num_added, 1)
                            dve.wait_ge(L.num_added, n + 1)

                def first_nodes(t, count):
                    _, vals = nc.values_load_multi_w_load_instructions(
                        base_row[0:1, bass.ds(t, count)], engines=(DVE_,), min_val=0, max_val=N,
                        skip_runtime_bounds_check_because=SORTED)
                    return vals

                def turn(c, front, soft, agg):
                    early = isinstance(c, int) and c == 2
                    if agg:
                        nodes = [None] * TG + list(first_nodes(0, TC - TG)) if early else first_nodes(c * TC - (2 * TC + TG), TC)
                    for g in range(GC):
                        n, s = c * GC + g, g % 2
                        if front:
                            dve.wait_ge(L.loaded[g], (c + 1) * 96)
                            above(dve, L.z_made, n - 1)
                            v.tensor_scalar(onehot[s][:, :], rel_bc[g][:, :], iota_col[:, 0:1], None, ALU.is_equal
                                            ).then_inc(L.onehot_made, 1)
                        if soft and g == 0:
                            masks(c - 1)
                        if soft and g == 1:
                            row_maxima(c - 1)
                        if soft and g == 2:
                            subtract_maxima(c - 1)
                        if soft and g == 3:
                            dve.wait_ge(L.soft_dve, (c - 1) * 6 + 4)
                            chain(c - 1, 4, SEND_F, SEND_B, ecar[0:1, 1:2], sumC, sumD, keepA, keepE, cont,
                                  ALU.mult, ALU.add, 0.0)
                        if agg:
                            if not (early and g == 0):
                                add_sums((c - 2) * GC + g - 1, (g - 1) % GC, nodes[g * TG:g * TG + TG])
                            if g == 0:
                                weight_cols(c - 2, nodes[TG])
                            weighted_onehot(c - 2, g)
                        if front:
                            if one:
                                dve.wait_ge(L.z_copied, n + 1)
                            else:
                                dve.wait_ge(L.z_made, n + 1)
                                v.tensor_tensor(zs[s][:, :], bZ[s][:, :], edge_in[g][:, :], ALU.add
                                                ).then_inc(L.z_used, 1)
                                dve.wait_ge(L.z_used, n + 1)
                            z = (zc if one else zs)[s]
                            above(dve, L.score_made, n - 1)
                            v.scalar_tensor_tensor(fT[s][:, :], z[:, :], SLOPE, z[:, :], ALU.mult, ALU.max
                                                   ).then_inc(L.f_made, 1)
                            if one:
                                above(dve, L.g2_made, n - 1)
                                v.scalar_tensor_tensor(zs[s][:, :], z[:, :], 0.0, edge_in[g][:, :],
                                                       ALU.max, ALU.add).then_inc(L.z_used, 1)
                        if soft and g == 1:
                            dve.wait_ge(L.soft_dve, (c - 1) * 6 + 1)
                            chain(c - 1, 2, END_F, END_B, None, rowC, rowD, penA, penE, penC,
                                  ALU.add, ALU.max, -BIG)
                        if soft and g == 2:
                            row_sums(c - 1)
                        if soft and g == 3:
                            normalise(c - 1)

                for c in range(3):
                    turn(c, True, c >= 1, c >= 2)
                start, step.k = step.k, 0
                with dve.Fori(0, CH - 3) as j:
                    step.base = j * STEPS + start
                    turn(j + 3, True, True, True)
                assert step.k == STEPS, step.k
                step.base, step.k = 0, start + (CH - 3) * STEPS
                turn(CH, False, True, True)
                turn(CH + 1, False, False, True)
                add_sums(NG - 1, GC - 1, first_nodes(NT - TG, TG))

            layer(L1)

            def middle(m, s, r):
                dve.wait_ge(m_in[s], (r + 1) * 16)
                dve.wait_ge(m_ht, m + 1)
                above(dve, m_rows, m - 1)
                v.scalar_tensor_tensor(zs[s][:, :], bZ[s][:, :], 0.0, slab[s][:, :], ALU.max, ALU.add
                                       ).then_inc(m_h0, 1)
                dve.wait_ge(m_rows, m + 1)
                above(dve, m_rows_stored[s], r * 16)
                v.tensor_copy(natB[s][:, :, :].rearrange("p b d -> p (b d)"), (bXT, bG2)[s][:, :]
                              ).then_inc(m_rows_copied, 1)

            slabs(dve, middle)
            v.memset(numT[:, :], 0.0).then_inc(m_zero, 1)
            dve.wait_ge(m_zero, 1)
            layer(L2)

            order = Steps(dve, e_dve)

            def end(m, s, r):
                order.base, order.k = m * END_STEPS, 0
                dve.wait_ge(e_in[s], (r + 1) * 16)
                dve.wait_ge(e_ht, m + 1)
                above(dve, e_rows, m - 1)
                v.scalar_tensor_tensor(zs[s][:, :], slab[s][:, :], 2.0, bZ[s][:, :], ALU.mult, ALU.add
                                       ).then_inc(e_y, 1)
                dve.wait_ge(e_rows, m + 1)
                for b in range(TG):
                    last = v.bn_stats(stats[:, b, :], bAG[s][:, b * P:b * P + P])
                order(last)
                dve.sem_inc(dve_passed, 1)
                for b in range(TG):
                    last = v.bn_aggr(mv[:, b, :], stats[:, b, :])
                order(last)
                v.tensor_scalar(std[:, :], mv[:, :, 1], EPS, None, ALU.add).then_inc(e_var, 1)
                dve.wait_ge(e_std, m + 1)
                order(v.reciprocal(rstd[:, :], std[:, :]))
                above(dve, e_stored[s], r * 16)
                for b in range(TG):
                    last = v.tensor_scalar(natA[s][:, b, :], bAG[s][:, b * P:b * P + P], mv[:, b, 0:1],
                                           rstd[:, b:b + 1], ALU.subtract, ALU.mult)
                last.then_inc(e_out, 1)

            slabs(dve, end)


END_STEPS = 3
STEPS = 29


def kernel(**inputs):
    import numpy as np
    import concourse.bacc as bacc
    from concourse import mybir as _mybir
    from concourse.bass_utils import run_bass_kernel_spmd as run

    x = np.asarray(inputs["x"])
    src = np.asarray(inputs["src"])
    dst = np.asarray(inputs["dst"])
    edges = np.asarray(inputs["edge_attr_128"])
    ep = NT * P
    srcp = np.concatenate([src, np.zeros(ep - E, src.dtype)])
    dstp = np.concatenate([dst, np.full(ep - E, N, dst.dtype)])
    edgep = np.concatenate([edges, np.zeros((ep - E, D), edges.dtype)])
    xp = np.concatenate([x, np.zeros((NP - N, D), x.dtype)])
    t = np.ascontiguousarray
    arrays = {
        "eT": t(edgep.reshape(NG, W, D).transpose(0, 2, 1)),
        "xT": t(xp.T),
        "xrows": t(x),
        "idxT": t(srcp.reshape(NT, P).T),
        "dstT": t(dstp.reshape(NT, P).T),
        "dstR": t(dstp.reshape(CH, TC, P).transpose(1, 0, 2)),
        "dst8": t(dstp.reshape(NT // 8, 8, P)),
        "ends": t(dstp.reshape(NT, P)[:, [0, P - 1]].T),
    }
    for layer in ("1", "2"):
        for w in ("fij", "ni", "nj", "node"):
            arrays[f"w_{w}{layer}"] = t(np.asarray(inputs[f"L0_gnn_W{layer}_{w}"]).T)
        arrays[f"attn{layer}"] = t(np.asarray(inputs[f"L0_gnn_attn{layer}"]).reshape(D, 1))
    nc = bacc.Bacc("TRN2", target_bir_lowering=False, num_devices=1)
    args = {n: nc.dram_tensor(n, a.shape, _mybir.dt.from_np(a.dtype), kind="ExternalInput").ap()
            for n, a in arrays.items()}
    out = nc.dram_tensor("out", (N, D), _mybir.dt.from_np(x.dtype), kind="ExternalOutput").ap()
    program(nc, out=out, **args)
    r = run(nc, [arrays], core_ids=[0])
    return r.results[0]["out"]
```

```python
import concourse.bass as bass
from concourse import mybir
from contextlib import ExitStack

N, E, D = 6250, 106250, 128
P = 128
TG = 4
GC = 8
GS = 4
AHEAD = 5
WIN = 64
TC = TG * GC
W = TG * P
CH = -(-E // (TC * P))
NT = CH * TC
NG = CH * GC
NS = -(-(N + P) // W)
NP = NS * W
XB = 3
BIG = 1e38
SLOPE = 0.2
EPS = 1e-5
SORTED = "dst lies in [0, N], its padding at N"


class Layer:

    def __init__(self, sem, n, edges_in, proj_dst, table, h1_out):
        self.n = n
        self.edges_in, self.proj_dst, self.table, self.h1_out = edges_in, proj_dst, table, h1_out
        self.loaded = [sem(f"loaded{n}_{g}") for g in range(GS)]
        self.gathered = [[sem(f"gathered{n}_{b}_{g}") for g in range(GC)] for b in range(XB)]
        self.idx_ready = sem(f"idx_ready{n}")
        self.xt_made = sem(f"xt_made{n}")
        self.xt_copied = sem(f"xt_copied{n}")
        self.onehot_made = sem(f"onehot_made{n}")
        self.z_made = sem(f"z_made{n}")
        self.z_copied = sem(f"z_copied{n}")
        self.f_made = sem(f"f_made{n}")
        self.score_made = sem(f"score_made{n}")
        self.score_copied = sem(f"score_copied{n}")
        self.h1_made = sem(f"h1_made{n}")
        self.h1_stored = [sem(f"h1_stored{n}_{g}") for g in range(GS)]
        self.soft_pe = sem(f"soft_pe{n}")
        self.soft_dve = sem(f"soft_dve{n}")
        self.soft_act = sem(f"soft_act{n}")
        self.a_made = sem(f"a_made{n}")
        self.num_made = sem(f"num_made{n}")
        self.num_added = sem(f"num_added{n}")
        self.dve_step = sem(f"dve_step{n}")


class Steps:

    def __init__(self, eng, sem):
        self.eng, self.sem, self.base, self.k = eng, sem, 0, 0

    def __call__(self, ins):
        self.k += 1
        ins.then_inc(self.sem, 1)
        self.eng.wait_ge(self.sem, self.base + self.k)


def above(eng, sem, value):
    if not isinstance(value, int) or value > 0:
        eng.wait_ge(sem, value)


def program(nc, eT, xT, xrows, idxT, dstT, dstR, dst8, ends, w_fij1, w_ni1, w_nj1, w_node1, attn1,
            w_fij2, w_ni2, w_nj2, w_node2, attn2, out):
    f32, bf16, i32 = mybir.dt.float32, mybir.dt.bfloat16, mybir.dt.int32
    ALU, ACT = mybir.AluOpType, mybir.ActivationFunctionType
    PE_, DVE_, SP_ = mybir.EngineType.PE, mybir.EngineType.DVE, mybir.EngineType.SP

    proj1 = nc.dram_tensor("proj1", [NP, D], f32, kind="Internal").ap()
    proj2 = nc.dram_tensor("proj2", [NP, D], f32, kind="Internal").ap()
    h0rows = nc.dram_tensor("h0rows", [NP, D], f32, kind="Internal").ap()
    h1T = nc.dram_tensor("h1T", [NG, P, W], f32, kind="Internal").ap()
    relrow = nc.dram_tensor("relrow", [NG, W], bf16, kind="Internal").ap()
    relrow_g = nc.dram_tensor("relrow_g", [NG, W], bf16, kind="Internal").ap()

    ctx = ExitStack()
    with ctx:
        def sb(name, shape, dt=f32):
            return ctx.enter_context(nc.sbuf_tensor(name, shape, dt))

        def pb(name):
            return ctx.enter_context(nc.psum_tensor(name, [P, W], f32))

        def sem(name):
            return ctx.enter_context(nc.semaphore(name))

        ident = sb("ident", [P, P])
        iota_row = sb("iota_row", [P, P])
        iota_col = sb("iota_col", [P, 1])
        ones = sb("ones", [P, P])
        wts = sb("wts", [P, 8, P])
        attn = sb("attn", [P, 2])
        attn_at = sb("attn_at", [P, 2, 2 * TC - 1])
        FIJ, NI, NJ, NODE = 0, 1, 2, 3

        idx_all = sb("idx_all", [P, NT], i32)
        dst_rows = sb("dst_rows", [TC, CH, P], i32)
        dst_col = sb("dst_col", [P, NT], i32)
        rel_col = sb("rel_col", [P, NT])
        base_all = sb("base_all", [P, NT], i32)
        fits = sb("fits", [1, 4], i32)
        span = sb("span", [1, NG])
        widest = sb("widest", [1, 1])
        base_row = sb("base_row", [1, NT], i32)
        last_row = sb("last_row", [1, NT], i32)
        group_row = sb("group_row", [1, NG], i32)
        cont = sb("cont", [1, NT + 1])
        whole = sb("whole", [1, NT + 1])
        keepA = sb("keepA", [1, NT + 1])
        keepE = sb("keepE", [1, NT + 1])
        penC = sb("penC", [1, NT + 1])
        penA = sb("penA", [1, NT + 1])
        penE = sb("penE", [1, NT + 1])
        dst8_t = sb("dst8_t", [NT // 8, 8, P], i32)
        rel8 = sb("rel8", [NT // 8, 8, P], bf16)
        rel8g = sb("rel8g", [NT // 8, 2, W], bf16)

        edge_in = [sb(f"edge_in{g}", [P, W]) for g in range(GS)]
        window = [sb(f"window{g}", [P, TG, P]) for g in range(GS)]
        rel_bc = [sb(f"rel_bc{g}", [P, W], bf16) for g in range(GS)]
        xsrc = [sb(f"xsrc{b}", [P, TC, P]) for b in range(XB)]
        idx_slot = [sb(f"idx_slot{b}", [P, TC], i32) for b in range(XB)]
        xsT = [sb(f"xsT{s}", [P, W]) for s in range(2)]
        onehot = [sb(f"onehot{s}", [P, W]) for s in range(2)]
        zc = [sb(f"zc{s}", [P, W]) for s in range(2)]
        h1 = [sb(f"h1_{s}", [P, W]) for s in range(GS)]
        fT = [sb(f"fT{s}", [P, W]) for s in range(2)]
        amat = [sb(f"amat{s}", [P, TG, P]) for s in range(2)]
        apair = [a[:, :, :].rearrange("p i (h j) -> p (i h) j", j=WIN) for a in amat]
        numT = sb("numT", [P, NP])

        score_sb = sb("score_sb", [TC, P])
        keep = sb("keep", [TC, P + 1])
        pen = sb("pen", [TC, P + 1])
        isF = sb("isF", [TC, P])
        isL = sb("isL", [TC, P])
        penF = sb("penF", [TC, P])
        penL = sb("penL", [TC, P])
        scanF = sb("scanF", [TC, P])
        scanB = sb("scanB", [TC, P])
        seg = sb("seg", [TC, P])
        aexp = sb("aexp", [TC, P])
        cd = sb("cd", [TC, 2])
        rowC = sb("rowC", [1, TC + 1])
        rowD = sb("rowD", [1, TC])
        sumC = sb("sumC", [1, TC + 1])
        sumD = sb("sumD", [1, TC])
        u1 = sb("u1", [1, TC])
        u2 = sb("u2", [1, TC])
        u3 = sb("u3", [1, TC])
        ecar = sb("ecar", [1, 2])
        cfac = sb("cfac", [1, 1])
        rcol = sb("rcol", [P, TC])
        wcol = sb("wcol", [P, TC + 1])
        relc = sb("relc", [P, TC])

        slab, zs = zc, h1[0:2]
        natA = [sb(f"natA{s}", [P, TG, P]) for s in range(2)]
        natB = [t[:, :].rearrange("p (b d) -> p b d", b=TG) for t in h1[2:4]]
        stats = sb("stats", [P, TG, 6])
        mv = sb("mv", [P, TG, 2])
        std = sb("std", [P, TG])
        rstd = sb("rstd", [P, TG])
        shift = sb("shift", [P, TG])

        bXT, bX2, bSC, bSM = pb("bXT"), pb("bX2"), pb("bSC"), pb("bSM")
        bZ = [pb("bZ0"), pb("bZ1")]
        bAG = [pb("bAG0"), pb("bAG1")]
        END_F, END_B = bSM[0:1, 128:128 + TC], bSM[0:1, 160:160 + TC]
        CD = bSM[0:TC, 192:194]
        SEND_F, SEND_B = bSM[0:1, 224:224 + TC], bSM[0:1, 256:256 + TC]
        SCD = bSM[0:TC, 288:290]
        ACOL, TCOL, CCOL = bSM[:, 320:320 + TC], bSM[:, 352:352 + TC], bSM[:, 384:385]

        pe_passed, dve_passed, pool_passed = sem("pe_passed"), sem("dve_passed"), sem("pool_passed")
        const_in = sem("const_in")
        idx_in = sem("idx_in")
        graph_in = sem("graph_in")
        rel8_in = sem("rel8_in")
        const_made = sem("const_made")
        iota_made = sem("iota_made")
        rel8_made = sem("rel8_made")
        rel_stored = sem("rel_stored")
        fits_made = sem("fits_made")
        attn_made = sem("attn_made")
        rel_made = sem("rel_made")
        dve_pro = sem("dve_pro")
        L1 = Layer(sem, 1, eT, proj1, xrows, h1T)
        L2 = Layer(sem, 2, h1T, proj2, h0rows, None)
        p_in = [sem("p_in0"), sem("p_in1")]
        p_made = sem("p_made")
        p_copied = sem("p_copied")
        p_stored = [sem("p_stored0"), sem("p_stored1")]
        m_in = [sem("m_in0"), sem("m_in1")]
        m_ht = sem("m_ht")
        m_h0 = sem("m_h0")
        m_zero = sem("m_zero")
        m_proj = sem("m_proj")
        m_rows = sem("m_rows")
        m_proj_copied = sem("m_proj_copied")
        m_rows_copied = sem("m_rows_copied")
        m_proj_stored = [sem("m_proj_stored0"), sem("m_proj_stored1")]
        m_rows_stored = [sem("m_rows_stored0"), sem("m_rows_stored1")]
        e_in = [sem("e_in0"), sem("e_in1")]
        e_ht = sem("e_ht")
        e_y = sem("e_y")
        e_rows = sem("e_rows")
        e_var = sem("e_var")
        e_std = sem("e_std")
        e_norm = sem("e_norm")
        e_out = sem("e_out")
        e_dve = sem("e_dve")
        e_stored = [sem("e_stored0"), sem("e_stored1")]

        block = ctx.enter_context(nc.Block())
        consts = [w_fij1, w_ni1, w_nj1, w_node1, w_fij2, w_ni2, w_nj2, w_node2]
        rows4 = lambda t, m: t[bass.ds(m * W, W), :].rearrange("(b p) d -> p b d", p=P)

        def slabs(eng, body):
            body(0, 0, 0)
            body(1, 1, 0)
            turns = NS // 2 - 1
            with eng.Fori(0, turns) as j:
                body(j * 2 + 2, 0, j + 1)
                body(j * 2 + 3, 1, j + 1)
            for m in range(2 + 2 * turns, NS):
                body(m, m % 2, m // 2)

        @block.sync
        def _(sp):
            sp.dma_start(dst8_t[:, :, :], dst8).then_inc(rel8_in, 16)
            sp.dma_start(base_all[:, :], ends[0:1, :].partition_broadcast(P)).then_inc(graph_in, 16)
            sp.dma_start(dst_col[:, :], dstT).then_inc(graph_in, 16)
            sp.dma_start(base_row[:, :], ends[0:1, :]).then_inc(graph_in, 16)
            sp.dma_start(last_row[:, :], ends[1:2, :]).then_inc(graph_in, 16)
            sp.dma_start(dst_rows[:, :, :], dstR).then_inc(graph_in, 16)

            def slab_in(arrived, used):
                def body(m, s, r):
                    above(sp, used, m - 1)
                    sp.dma_start(slab[s][:, :], xT[:, bass.ds(m * W, W)]).then_inc(arrived[s], 16)
                return body

            slab_p = slab_in(p_in, p_made)
            slabs(sp, slab_p)

            sp.wait_ge(rel8_made, 1)
            sp.dma_start(relrow.rearrange("(p a) w -> p (a w)", a=2),
                         rel8[:, :, :].rearrange("p a e -> p (a e)")).then_inc(rel_stored, 16)
            sp.dma_start(relrow_g.rearrange("(p a) w -> p (a w)", a=2),
                         rel8g[:, :, :].rearrange("p a e -> p (a e)")).then_inc(rel_stored, 16)
            sp.wait_ge(rel_stored, 32)

            def load_layer(L, narrow):
                def first_nodes(row, at, count):
                    _, first = nc.values_load_multi_w_load_instructions(
                        row[0:1, bass.ds(at, count)], engines=(SP_,), min_val=0, max_val=N,
                        skip_runtime_bounds_check_because=SORTED)
                    return first

                def chunk(c):
                    if narrow:
                        first = first_nodes(group_row, c * GC, GC)
                    for g in range(GC):
                        n, q = c * GC + g, g % GS
                        above(sp, L.z_made, n - (GS - 1))
                        if L.h1_out is not None:
                            above(sp, L.h1_made, n - (GS - 1))
                        sp.dma_start(edge_in[q][:, :], L.edges_in[bass.ds(n, 1), :, :].rearrange(
                            "o p w -> (o p) w")).then_inc(L.loaded[q], 16)
                        if narrow:
                            sp.dma_start(rel_bc[q][0:WIN, :], relrow_g[bass.ds(n, 1), :].partition_broadcast(WIN)
                                         ).then_inc(L.loaded[q], 16)
                            sp.dma_start(window[q][0:WIN, 0, :], L.proj_dst[bass.ds(first[g], WIN), :]
                                         ).then_inc(L.loaded[q], 16)
                        else:
                            first = first_nodes(base_row, n * TG, TG)
                            sp.dma_start(rel_bc[q][:, :], relrow[bass.ds(n, 1), :].partition_broadcast(P)
                                         ).then_inc(L.loaded[q], 16)
                            for i in range(TG):
                                sp.dma_start(window[q][:, i, :],
                                             L.proj_dst[bass.ds(first[i], P), :]
                                             ).then_inc(L.loaded[q], 16)
                        if L.h1_out is not None and not (isinstance(c, int) and n < GS):
                            store_h1(L, n - GS, q)
                return chunk

            def store_h1(L, n, q):
                sp.wait_ge(L.h1_made, n + 1)
                sp.dma_start(L.h1_out[bass.ds(n, 1), :, :].rearrange("o p w -> (o p) w"), h1[q][:, :]
                             ).then_inc(L.h1_stored[q], 16)

            def layer(L, narrow):
                chunk = load_layer(L, narrow)
                chunk(0)
                with sp.Fori(1, CH) as c:
                    chunk(c)
                if L.h1_out is not None:
                    for n in range(NG - GS, NG):
                        store_h1(L, n, n % GS)
                    for q in range(GS):
                        sp.wait_ge(L.h1_stored[q], 16 * (NG // GS))

            sp.wait_ge(fits_made, 1)
            fit = nc.sync.value_load(fits[0:1, 0:1], min_val=0, max_val=1)

            def either(L):
                with sp.If(fit == 1):
                    layer(L, True)
                with sp.Else():
                    layer(L, False)

            for s in range(2):
                sp.wait_ge(p_stored[s], 16 * ((NS + 1 - s) // 2))
            sp.wait_ge(graph_in, 16 * 5)
            either(L1)

            slab_m = slab_in(m_in, m_h0)

            def middle(m, s, r):
                slab_m(m, s, r)
                if not isinstance(m, int) or m >= 1:
                    rows_out(m - 1, 1 - s)

            def rows_out(m, s):
                sp.wait_ge(m_rows_copied, m + 1)
                sp.dma_start(rows4(h0rows, m), natB[s][:, :, :]).then_inc(m_rows_stored[s], 16)

            slabs(sp, middle)
            rows_out(NS - 1, (NS - 1) % 2)
            for s in range(2):
                sp.wait_ge(m_rows_stored[s], 16 * ((NS + 1 - s) // 2))
                sp.wait_ge(m_proj_stored[s], 16 * ((NS + 1 - s) // 2))
            either(L2)
            sp.wait_ge(L2.f_made, NG)

            slab_e = slab_in(e_in, e_y)

            def end(m, s, r):
                slab_e(m, s, r)
                if not isinstance(m, int) or m >= 1:
                    y_out(m - 1, 1 - s)

            def y_out(m, s):
                sp.wait_ge(e_out, m + 1)
                sp.dma_start(rows4(out, m), natA[s][:, :, :]).then_inc(e_stored[s], 16)

            slabs(sp, end)
            m, s = NS - 1, (NS - 1) % 2
            sp.wait_ge(e_out, m + 1)
            sp.dma_start(out[m * W:N, :], natA[s][0:N - m * W, 0, :]).then_inc(e_stored[s], 16)
            for s in range(2):
                sp.wait_ge(e_stored[s], 16 * ((NS + 1 - s) // 2))

        @block.gpsimd
        def _(pool):
            pool.dma_start(idx_all[:, :], idxT).then_inc(idx_in, 16)
            nc.gpsimd.iota(iota_row[:, :], [[1, P]], base=0, channel_multiplier=0,
                           allow_small_or_imprecise_dtypes=True).then_inc(iota_made, 1)
            nc.gpsimd.iota(iota_col[:, :], [[0, 1]], base=0, channel_multiplier=1,
                           allow_small_or_imprecise_dtypes=True).then_inc(iota_made, 1)
            nc.gpsimd.memset(ones[:, :], 1.0).then_inc(iota_made, 1)
            pool.wait_ge(iota_made, 3)
            nc.gpsimd.affine_select(out=ident[:, :], in_=ones[:, :], compare_op=ALU.is_equal, fill=0.0,
                                    base=0, pattern=[[-1, P]], channel_multiplier=1).then_inc(const_made, 1)
            pool.wait_ge(idx_in, 16)

            def layer(L):
                def chunk(c, b, again):
                    if again:
                        pool.wait_ge(L.num_made, (c - XB) * GC + 1)
                    nc.gpsimd.tensor_copy(idx_slot[b][:, :], idx_all[:, bass.ds(c * TC, TC)]
                                          ).then_inc(L.idx_ready, 1)
                    pool.wait_ge(L.idx_ready, c + 1)
                    pool.sem_inc(pool_passed, 1)
                    for g in range(GC):
                        if again:
                            pool.wait_ge(L.num_made, (c - XB) * GC + g + 1)
                            pool.sem_inc(pool_passed, 1)
                        for i in range(g * TG, g * TG + TG):
                            pool.indirect_dma_start(
                                xsrc[b][:, i, :], None, L.table,
                                bass.IndirectOffsetOnAxis(ap=idx_slot[b][:, i:i + 1], axis=0)
                            ).then_inc(L.gathered[b][g], 16)

                for c in range(XB):
                    chunk(c, c, False)
                turns = (CH - XB) // XB
                with pool.Fori(0, turns) as j:
                    for b in range(XB):
                        chunk(j * XB + (XB + b), b, True)
                for c in range(XB + turns * XB, CH):
                    chunk(c, c % XB, True)

            layer(L1)
            for s in range(2):
                pool.wait_ge(m_rows_stored[s], 16 * ((NS + 1 - s) // 2))
            layer(L2)

        @block.scalar
        def _(act):
            for k, w in enumerate(consts):
                act.dma_start(wts[:, k, :], w).then_inc(const_in, 16)
            act.dma_start(attn[:, 0:1], attn1).then_inc(const_in, 16)
            act.dma_start(attn[:, 1:2], attn2).then_inc(const_in, 16)

            def project(m, s, r):
                act.wait_ge(p_made, m + 1)
                above(act, p_stored[s], r * 16)
                nc.scalar.copy(natA[s][:, :, :].rearrange("p b d -> p (b d)"), bAG[s][:, :]).then_inc(p_copied, 1)
                act.wait_ge(p_copied, m + 1)
                act.dma_start(rows4(proj1, m), natA[s][:, :, :]).then_inc(p_stored[s], 16)

            slabs(act, project)

            def layer(L):
                def slot(c, g, front, soft):
                    n, s = c * GC + g, g % 2
                    if soft and g == 3:
                        act.wait_ge(L.soft_dve, (c - 1) * 6 + 3)
                        nc.scalar.activation(aexp[:, :], seg[:, :], ACT.Exp)
                        nc.scalar.activation(ecar[0:1, 1:2], ecar[0:1, 0:1], ACT.Exp).then_inc(L.soft_act, 1)
                    if front:
                        act.wait_ge(L.z_made, n + 1)
                        above(act, L.f_made, n - 1)
                        if L.h1_out is not None:
                            above(act, L.h1_made, n - 1)
                        nc.scalar.copy(zc[s][:, :], bZ[s][:, :]).then_inc(L.z_copied, 1)
                    if g == 0 and soft:
                        act.wait_ge(L.score_made, c * GC)
                        above(act, L.soft_dve, (c - 1) * 6 - 3)
                        nc.scalar.copy(score_sb[:, :], bSC[0:TC, 0:P]).then_inc(L.score_copied, 1)
                    if front and not (isinstance(c, int) and n == NG - 1):
                        copy_rows(n + 1, 1 - s)

                def copy_rows(n, s):
                    act.wait_ge(L.xt_made, n + 1)
                    above(act, L.z_made, n - 1)
                    nc.scalar.copy(xsT[s][:, :], bXT[:, :]).then_inc(L.xt_copied, 1)

                def turn(c, front, soft):
                    for g in range(GC):
                        slot(c, g, front, soft)

                copy_rows(0, 0)
                turn(0, True, False)
                turn(1, True, True)
                with act.Fori(2, CH - 1) as c:
                    turn(c, True, True)
                turn(CH - 1, True, True)
                turn(CH, False, True)

            layer(L1)

            def middle(m, s, r):
                act.wait_ge(m_proj, m + 1)
                above(act, m_proj_stored[s], r * 16)
                nc.scalar.copy(natA[s][:, :, :].rearrange("p b d -> p (b d)"), bAG[s][:, :]
                               ).then_inc(m_proj_copied, 1)
                act.wait_ge(m_proj_copied, m + 1)
                act.dma_start(rows4(proj2, m), natA[s][:, :, :]).then_inc(m_proj_stored[s], 16)

            slabs(act, middle)
            layer(L2)

            def end(m, s, r):
                act.wait_ge(e_var, m + 1)
                nc.scalar.activation(std[:, :], std[:, :], ACT.Sqrt).then_inc(e_std, 1)
                act.wait_ge(e_norm, m + 1)
                above(act, e_stored[s], r * 16)
                for b in range(TG):
                    last = nc.scalar.activation(natA[s][:, b, :], bAG[s][:, b * P:b * P + P], ACT.Identity,
                                                bias=shift[:, b:b + 1], scale=rstd[:, b:b + 1])
                last.then_inc(e_out, 1)

            slabs(act, end)

        @block.tensor
        def _(pe):
            mm, tp = nc.tensor.matmul, nc.tensor.transpose
            pe.wait_ge(const_made, 1)
            pe.wait_ge(const_in, 16 * 10)

            def project(m, s, r):
                pe.wait_ge(p_in[s], (r + 1) * 16)
                above(pe, p_copied, m - 1)
                for b in range(TG):
                    last = mm(bAG[s][:, b * P:b * P + P], slab[s][:, b * P:b * P + P], wts[:, NJ, :],
                              start=True, stop=True)
                last.then_inc(p_made, 1)

            slabs(pe, project)

            def layer(L, narrow):
                ready = 48 if narrow else 96
                fij, ni = wts[:, (L.n - 1) * 4 + FIJ, :], wts[:, (L.n - 1) * 4 + NI, :]

                def transposed_rows(c, g, b, rounds):
                    n, s = c * GC + g, g % 2
                    if g == 0:
                        pe.wait_ge(L.gathered[b][AHEAD], (rounds + 1) * 16 * TG)
                    pe.wait_ge(L.gathered[b][g], (rounds + 1) * 16 * TG)
                    above(pe, L.xt_copied, n)
                    for i in range(TG):
                        last = tp(bXT[:, i * P:i * P + P], xsrc[b][:, g * TG + i, :], ident[:, :])
                    last.then_inc(L.xt_made, 1)

                def z_sum(c, g):
                    n, s, q = c * GC + g, g % 2, g % GS
                    above(pe, L.z_copied, n - 1)
                    pe.wait_ge(L.loaded[q], (c * (GC // GS) + g // GS + 1) * ready)
                    mm(bZ[s][:, :], fij, edge_in[q][:, :], start=True, stop=False)
                    pe.wait_ge(L.onehot_made, n + 1)
                    if narrow:
                        mm(bZ[s][:, :], window[q][0:WIN, 0, :], onehot[s][0:WIN, :], start=False, stop=False)
                    else:
                        for i in range(TG):
                            mm(bZ[s][:, i * P:i * P + P], window[q][:, i, :], onehot[s][:, i * P:i * P + P],
                               start=False, stop=False, skip_group_check=True)
                    pe.wait_ge(L.xt_copied, n + 1)
                    last = mm(bZ[s][:, :], ni, xsT[s][:, :], start=False, stop=True, skip_group_check=not narrow)
                    last.then_inc(L.z_made, 1)

                def scores(c, g):
                    n, s = c * GC + g, g % 2
                    pe.wait_ge(L.f_made, n + 1)
                    if g == 0:
                        above(pe, L.score_copied, c)
                    for i in range(TG):
                        t = g * TG + i
                        last = mm(bSC[0:TC, 0:P], attn_at[:, L.n - 1, TC - 1 - t:2 * TC - 1 - t],
                                  fT[s][:, i * P:i * P + P], start=t == 0, stop=t == TC - 1)
                    last.then_inc(L.score_made, 1)

                def partial(k, g, b):
                    n, s = k * GC + g, g % 2
                    if narrow:
                        pe.wait_ge(L.a_made, k * (GC // 2) + g // 2 + 1)
                    else:
                        pe.wait_ge(L.a_made, n + 1)
                    above(pe, L.num_added, n - 1)
                    for i in range(TG):
                        rows = xsrc[b][:, g * TG + i, :]
                        if narrow:
                            last = mm(bAG[s][:, 0:WIN], rows, apair[g // 2 % 2][:, g % 2 * TG + i, :],
                                      start=i == 0, stop=i == TG - 1)
                        else:
                            last = mm(bAG[s][:, i * P:i * P + P], rows, amat[s][:, i, :], start=True, stop=True)
                    last.then_inc(L.num_made, 1)

                def ends_to_row(k, step, f, b):
                    pe.wait_ge(L.soft_dve, k * 6 + step)
                    pe.sem_inc(pe_passed, 1)
                    tp(f, scanF[:, P - 1:P], ident[0:TC, 0:TC])
                    tp(b, scanB[:, 0:1], ident[0:TC, 0:TC]).then_inc(L.soft_pe, 1)

                def row_to_cols(k, step, cols, c_row, d_row):
                    pe.wait_ge(L.soft_dve, k * 6 + step)
                    pe.sem_inc(pe_passed, 1)
                    tp(cols[:, 0:1], c_row[0:1, 0:TC], ident[0:1, 0:1])
                    tp(cols[:, 1:2], d_row[0:1, 0:TC], ident[0:1, 0:1]).then_inc(L.soft_pe, 1)

                def weights_to_cols(k):
                    pe.wait_ge(L.soft_dve, k * 6 + 6)
                    pe.sem_inc(pe_passed, 1)
                    tp(ACOL, aexp[:, :], ident[0:TC, 0:TC])
                    tp(TCOL, seg[:, :], ident[0:TC, 0:TC])
                    mm(CCOL, ones[0:1, :], cfac[0:1, 0:1], start=True, stop=True).then_inc(L.soft_pe, 1)

                def turn(c, b, rounds, has_front, soft, agg, has_next=True):
                    for g in range(GC):
                        if has_front:
                            z_sum(c, g)
                        if g == 0:
                            if soft:
                                scores(c - 1, GC - 1)
                        elif has_front:
                            scores(c, g - 1)
                        if has_front and g < GC - 1:
                            transposed_rows(c, g + 1, b, rounds)
                        elif has_front and has_next:
                            transposed_rows(c + 1, 0, (b + 1) % XB, rounds + (b + 1) // XB)
                        if agg:
                            partial(c - 2, g, (b - 2) % XB)
                        if soft:
                            if g == 1:
                                ends_to_row(c - 1, 1, END_F, END_B)
                            if g == 2:
                                row_to_cols(c - 1, 2, CD, rowC, rowD)
                            if g == 4:
                                ends_to_row(c - 1, 4, SEND_F, SEND_B)
                            if g == 5:
                                row_to_cols(c - 1, 5, SCD, sumC, sumD)
                            if g == 6:
                                weights_to_cols(c - 1)

                transposed_rows(0, 0, 0, 0)
                for c in range(XB):
                    turn(c, c, 0, True, c >= 1, c >= 2)
                turns = (CH - XB) // XB
                with pe.Fori(0, turns) as j:
                    for b in range(XB):
                        turn(j * XB + (XB + b), b, j + 1, True, True, True)
                for c in range(XB + turns * XB, CH + 2):
                    turn(c, c % XB, c // XB, c < CH, c <= CH, True, c < CH - 1)

            pe.wait_ge(attn_made, 2)
            pe.wait_ge(fits_made, 1)
            fit = nc.tensor.value_load(fits[0:1, 0:1], min_val=0, max_val=1)

            def either(L):
                with pe.If(fit == 1):
                    layer(L, True)
                with pe.Else():
                    layer(L, False)

            either(L1)

            def node_sum(made, used, node, m, s):
                above(pe, used, m - 1)
                mm(bZ[s][:, :], node, numT[:, bass.ds(m * W, W)], start=True, stop=True).then_inc(made, 1)

            def middle_rest(m, s):
                pe.wait_ge(m_h0, m + 1)
                above(pe, m_proj_copied, m - 1)
                for b in range(TG):
                    last = mm(bAG[s][:, b * P:b * P + P], zs[s][:, b * P:b * P + P], wts[:, 4 + NJ, :],
                              start=True, stop=True)
                last.then_inc(m_proj, 1)
                bank = (bXT, bX2)[s]
                above(pe, m_rows_copied, m - 1)
                for b in range(TG):
                    last = tp(bank[:, b * P:b * P + P], zs[s][:, b * P:b * P + P], ident[:, :])
                last.then_inc(m_rows, 1)

            def middle(m, s, r):
                node_sum(m_ht, m_h0, wts[:, NODE, :], m, s)
                if not isinstance(m, int) or m >= 1:
                    middle_rest(m - 1, 1 - s)

            pe.wait_ge(L1.num_added, NG)
            slabs(pe, middle)
            middle_rest(NS - 1, (NS - 1) % 2)

            either(L2)

            def end_rest(m, s):
                pe.wait_ge(e_y, m + 1)
                above(pe, e_out, m - 1)
                for b in range(TG):
                    last = tp(bAG[s][:, b * P:b * P + P], zs[s][:, b * P:b * P + P], ident[:, :])
                last.then_inc(e_rows, 1)

            def end(m, s, r):
                node_sum(e_ht, e_y, wts[:, 4 + NODE, :], m, s)
                if not isinstance(m, int) or m >= 1:
                    end_rest(m - 1, 1 - s)

            pe.wait_ge(L2.num_added, NG)
            slabs(pe, end)
            end_rest(NS - 1, (NS - 1) % 2)

        @block.vector
        def _(dve):
            v = nc.vector
            step = Steps(dve, dve_pro)
            dve.wait_ge(rel8_in, 16)
            v.tensor_tensor(rel8[:, :, :], dst8_t[:, :, :], dst8_t[:, :, 0:1].broadcast_to((NT // 8, 8, P)),
                            ALU.subtract)
            by_group = dst8_t[:, :, :].rearrange("p (a i) e -> p a (i e)", a=2)
            v.tensor_tensor(rel8g[:, :, :], by_group, by_group[:, :, 0:1].broadcast_to((NT // 8, 2, W)),
                            ALU.subtract).then_inc(rel8_made, 1)
            v.memset(numT[:, :], 0.0)
            v.memset(keep[:, :], 0.0)
            step(v.memset(pen[:, :], 0.0))
            dve.wait_ge(graph_in, 16 * 5)
            v.tensor_copy(group_row[0:1, :], base_row[0:1, ::TG])
            v.memset(fits[:, :], 0)
            step(v.tensor_tensor(span[0:1, :], last_row[0:1, TG - 1::TG], base_row[0:1, ::TG], ALU.subtract))
            step(v.tensor_reduce(widest[0:1, :], span[0:1, :], mybir.AxisListType.X, ALU.max))
            v.tensor_scalar(fits[0:1, 0:1], widest[0:1, :], WIN - 0.5, None, ALU.is_lt).then_inc(fits_made, 1)
            v.memset(cont[:, :], 0.0)
            v.memset(whole[:, :], 0.0)
            v.memset(keepA[:, :], 0.0)
            step(v.memset(keepE[:, :], 0.0))
            v.tensor_tensor(cont[0:1, 1:NT], base_row[0:1, 1:NT], last_row[0:1, 0:NT - 1], ALU.is_equal)
            step(v.tensor_tensor(whole[0:1, 0:NT], base_row[0:1, :], last_row[0:1, :], ALU.is_equal))
            v.tensor_tensor(keepA[0:1, 1:NT + 1], cont[0:1, 1:NT + 1], whole[0:1, 0:NT], ALU.mult)
            step(v.tensor_tensor(keepE[0:1, :], cont[0:1, :], whole[0:1, :], ALU.mult))
            v.tensor_scalar(penC[0:1, :], cont[0:1, :], BIG, -BIG, ALU.mult, ALU.add)
            v.tensor_scalar(penA[0:1, :], keepA[0:1, :], BIG, -BIG, ALU.mult, ALU.add)
            step(v.tensor_scalar(penE[0:1, :], keepE[0:1, :], BIG, -BIG, ALU.mult, ALU.add))
            dve.wait_ge(iota_made, 3)
            dve.wait_ge(const_in, 16 * 10)
            v.memset(attn_at[:, :, :], 0.0).then_inc(attn_made, 1)
            dve.wait_ge(attn_made, 1)
            v.tensor_copy(attn_at[:, :, TC - 1], attn[:, :]).then_inc(attn_made, 1)
            dve.wait_ge(fits_made, 1)
            fit = v.value_load(fits[0:1, 0:1], min_val=0, max_val=1)

            def layer(L, narrow):
                one = L.h1_out is not None
                step = Steps(dve, L.dve_step)
                ready = 48 if narrow else 96

                cols = lambda a: a[:, :].rearrange("p (n i) -> p n i", i=TG if narrow else 1)
                v.tensor_tensor(cols(rel_col), cols(dst_col), cols(base_all)[:, :, 0:1].broadcast_to(
                    tuple(cols(dst_col).shape)), ALU.subtract)
                v.memset(rowC[:, :], -BIG)
                v.memset(sumC[:, :], 0.0)
                v.memset(sumD[:, :], 0.0)
                step(v.memset(rowD[:, :], -BIG))

                def masks(k):
                    d = dst_rows[:, k, :]
                    v.tensor_tensor(keep[:, 1:P], d[:, 1:P], d[:, 0:P - 1], ALU.is_equal)
                    v.tensor_tensor(isF[:, :], d, d[:, 0:1].broadcast_to((TC, P)), ALU.is_equal)
                    step(v.tensor_tensor(isL[:, :], d, d[:, P - 1:P].broadcast_to((TC, P)), ALU.is_equal))
                    v.tensor_scalar(pen[:, 1:P], keep[:, 1:P], BIG, -BIG, ALU.mult, ALU.add)
                    v.tensor_scalar(penF[:, :], isF[:, :], BIG, -BIG, ALU.mult, ALU.add)
                    step(v.tensor_scalar(penL[:, :], isL[:, :], BIG, -BIG, ALU.mult, ALU.add))

                def row_maxima(k):
                    dve.wait_ge(L.score_copied, k + 1)
                    v.tensor_tensor_scan(scanF[:, :], pen[:, 0:P], score_sb[:, :], -BIG, ALU.add, ALU.max)
                    step(v.tensor_tensor_scan(scanB[:, ::-1], pen[:, P:0:-1], score_sb[:, ::-1], -BIG, ALU.add, ALU.max))
                    v.tensor_tensor(seg[:, :], scanF[:, :], scanB[:, :], ALU.max).then_inc(L.soft_dve, 1)

                def chain(k, at, ends_f, ends_b, from_before, row, back, pa, pe_, pc, op0, op1, last):
                    dve.wait_ge(L.soft_pe, k * 5 + at - 1)
                    v.tensor_tensor(u1[0:1, :], ends_f, pc[0:1, bass.ds(k * TC + 1, TC)], op0)
                    if from_before is None:
                        v.tensor_copy(row[0:1, 0:1], row[0:1, TC:TC + 1])
                    else:
                        v.tensor_tensor(row[0:1, 0:1], row[0:1, TC:TC + 1], from_before, ALU.mult)
                    v.tensor_copy(u3[0:1, 0:TC - 1], pe_[0:1, bass.ds(k * TC + 1, TC - 1)])
                    step(v.tensor_tensor(u2[0:1, 0:TC - 1], ends_b[0:1, 1:TC], pc[0:1, bass.ds(k * TC + 1, TC - 1)],
                                         op0))
                    v.tensor_tensor_scan(row[0:1, 1:TC + 1], pa[0:1, bass.ds(k * TC + 1, TC)], u1[0:1, :],
                                         row[0:1, 0:1], op0, op1)
                    v.tensor_tensor_scan(back[0:1, TC - 2::-1], u3[0:1, TC - 2::-1],
                                         u2[0:1, TC - 2::-1], last, op0, op1).then_inc(L.soft_dve, 1)

                def subtract_maxima(k):
                    dve.wait_ge(L.soft_pe, k * 5 + 2)
                    dve.wait_ge(L.soft_dve, k * 6 + 2)
                    step(v.tensor_copy(cd[:, :], CD))
                    step(v.scalar_tensor_tensor(seg[:, :], penF[:, :], cd[:, 0:1], seg[:, :], ALU.add, ALU.max))
                    step(v.scalar_tensor_tensor(seg[:, :], penL[:, :], cd[:, 1:2], seg[:, :], ALU.add, ALU.max))
                    step(v.tensor_tensor(ecar[0:1, 0:1], rowC[0:1, 0:1], seg[0:1, 0:1], ALU.subtract))
                    v.tensor_tensor(seg[:, :], score_sb[:, :], seg[:, :], ALU.subtract).then_inc(L.soft_dve, 1)

                def row_sums(k):
                    dve.wait_ge(L.soft_act, k + 1)
                    v.tensor_tensor_scan(scanF[:, :], keep[:, 0:P], aexp[:, :], 0.0, ALU.mult, ALU.add)
                    step(v.tensor_tensor_scan(scanB[:, ::-1], keep[:, P:0:-1], aexp[:, ::-1], 0.0, ALU.mult, ALU.add))
                    step(v.tensor_tensor(seg[:, :], scanF[:, :], aexp[:, :], ALU.subtract))
                    v.tensor_tensor(seg[:, :], seg[:, :], scanB[:, :], ALU.add).then_inc(L.soft_dve, 1)

                def normalise(k):
                    dve.wait_ge(L.soft_pe, k * 5 + 4)
                    dve.wait_ge(L.soft_dve, k * 6 + 5)
                    step(v.tensor_copy(cd[:, :], SCD))
                    step(v.scalar_tensor_tensor(seg[:, :], isF[:, :], cd[:, 0:1], seg[:, :], ALU.mult, ALU.add))
                    step(v.scalar_tensor_tensor(seg[:, :], isL[:, :], cd[:, 1:2], seg[:, :], ALU.mult, ALU.add))
                    step(v.reciprocal(cfac[0:1, 0:1], seg[0:1, 0:1]))
                    v.tensor_tensor(cfac[0:1, 0:1], sumC[0:1, 0:1], cfac[0:1, 0:1], ALU.mult
                                    ).then_inc(L.soft_dve, 1)

                def weight_cols(k):
                    dve.wait_ge(L.soft_pe, k * 5 + 5)
                    v.tensor_copy(relc[:, :], rel_col[:, bass.ds(k * TC, TC)])
                    v.tensor_copy(wcol[:, TC:TC + 1], CCOL)
                    step(v.reciprocal(rcol[:, :], TCOL))
                    step(v.tensor_tensor(wcol[:, 0:TC], ACOL, rcol[:, :], ALU.mult))

                def rescale(base):
                    col = numT[:, bass.ds(base, 1)]
                    step(v.tensor_scalar(col, col, wcol[:, TC:TC + 1], None, ALU.mult))

                def weighted_onehot(k, g):
                    n, s = k * GC + g, g % 2
                    if narrow:
                        a, both = apair[g // 2 % 2], (P, 2 * TG, WIN)
                        of = lambda cols: cols[:, g * TG:(g + 2) * TG].unsqueeze(2).broadcast_to(both)
                        above(dve, L.num_made, n - 2)
                        step(v.tensor_tensor(a, iota_row[:, 0:WIN].unsqueeze(1).broadcast_to(both), of(relc),
                                             ALU.is_equal))
                        v.tensor_tensor(a, a, of(wcol), ALU.mult).then_inc(L.a_made, 1)
                        return
                    above(dve, L.num_made, n - 1)
                    for i in range(TG):
                        t = g * TG + i
                        last = v.tensor_scalar(amat[s][:, i, :], iota_row[:, :], relc[:, t:t + 1], wcol[:, t:t + 1],
                                               ALU.is_equal, ALU.mult)
                    last.then_inc(L.a_made, 1)

                def add_sums(n, g, node=None):
                    nodes = [node] if narrow else first_nodes(base_row, n * TG, TG)
                    dve.wait_ge(L.num_made, n + 1)
                    for i, node in enumerate(nodes):
                        w = WIN if narrow else P
                        win = numT[:, bass.ds(node, w)]
                        ins = v.tensor_tensor(win, win, bAG[g % 2][:, i * P:i * P + w], ALU.add)
                        if i < len(nodes) - 1:
                            step(ins)
                        else:
                            ins.then_inc(L.num_added, 1)
                            dve.wait_ge(L.num_added, n + 1)

                def first_nodes(row, at, count):
                    _, vals = nc.values_load_multi_w_load_instructions(
                        row[0:1, bass.ds(at, count)], engines=(DVE_,), min_val=0, max_val=N,
                        skip_runtime_bounds_check_because=SORTED)
                    return vals

                def one_hot(c, g):
                    n, s, q, w = c * GC + g, g % 2, g % GS, WIN if narrow else P
                    dve.wait_ge(L.loaded[q], (c * (GC // GS) + g // GS + 1) * ready)
                    above(dve, L.z_made, n - 1)
                    v.tensor_scalar(onehot[s][0:w, :], rel_bc[q][0:w, :], iota_col[0:w, 0:1], None,
                                    ALU.is_equal).then_inc(L.onehot_made, 1)

                def turn(c, front, soft, agg):
                    early = isinstance(c, int) and c == 2
                    if agg:
                        if narrow:
                            nodes = ([None] * TG + list(first_nodes(group_row, 0, GC)) if early else
                                     first_nodes(group_row, c * GC - (2 * GC + TG), GC + TG))[TG - 1:]
                        else:
                            nodes = [None] + list(first_nodes(group_row, c * GC - 2 * GC, TG)) + [None] * GC
                    for g in range(GC):
                        n, s, q = c * GC + g, g % 2, g % GS
                        if front and not (isinstance(c, int) and n == NG - 1):
                            one_hot(c, g + 1)
                        if soft:
                            if g == 0:
                                masks(c - 1)
                            if g == 1:
                                row_maxima(c - 1)
                            if g == 2:
                                dve.wait_ge(L.soft_dve, (c - 1) * 6 + 1)
                                chain(c - 1, 2, END_F, END_B, None, rowC, rowD, penA, penE, penC,
                                      ALU.add, ALU.max, -BIG)
                            if g == 3:
                                subtract_maxima(c - 1)
                            if g == 4:
                                row_sums(c - 1)
                            if g == 5:
                                dve.wait_ge(L.soft_dve, (c - 1) * 6 + 4)
                                chain(c - 1, 4, SEND_F, SEND_B, ecar[0:1, 1:2], sumC, sumD, keepA, keepE, cont,
                                      ALU.mult, ALU.add, 0.0)
                            if g == 6:
                                normalise(c - 1)
                        if agg:
                            if not (early and g == 0):
                                add_sums((c - 2) * GC + g - 1, (g - 1) % 2, nodes[g])
                            if g == 0:
                                rescale(nodes[1])
                            if not narrow:
                                weighted_onehot(c - 2, g)
                            elif g % 2 == 1 and g < GC - 1:
                                weighted_onehot(c - 2, g + 1)
                        if soft and g == GC - 1:
                            weight_cols(c - 1)
                            if narrow:
                                weighted_onehot(c - 1, 0)
                        if front:
                            dve.wait_ge(L.z_copied, n + 1)
                            above(dve, L.score_made, n - 1)
                            v.scalar_tensor_tensor(fT[s][:, :], zc[s][:, :], SLOPE, zc[s][:, :], ALU.mult, ALU.max
                                                   ).then_inc(L.f_made, 1)
                            if one:
                                above(dve, L.h1_stored[q], (c * (GC // GS) + g // GS) * 16)
                                v.scalar_tensor_tensor(h1[q][:, :], zc[s][:, :], 0.0, edge_in[q][:, :],
                                                       ALU.max, ALU.add).then_inc(L.h1_made, 1)

                one_hot(0, 0)
                for c in range(3):
                    turn(c, True, c >= 1, c >= 2)
                start, step.k = step.k, 0
                with dve.Fori(0, CH - 4) as j:
                    step.base = j * STEPS[narrow] + start
                    turn(j + 3, True, True, True)
                assert step.k == STEPS[narrow], step.k
                step.base, step.k = 0, start + (CH - 4) * STEPS[narrow]
                turn(CH - 1, True, True, True)
                turn(CH, False, True, True)
                turn(CH + 1, False, False, True)
                add_sums(NG - 1, 1, first_nodes(group_row, NG - TG, TG)[TG - 1])

            def either(L):
                with dve.If(fit == 1):
                    layer(L, True)
                with dve.Else():
                    layer(L, False)

            either(L1)

            def middle(m, s, r):
                dve.wait_ge(m_in[s], (r + 1) * 16)
                dve.wait_ge(m_ht, m + 1)
                above(dve, m_rows, m - 1)
                v.scalar_tensor_tensor(zs[s][:, :], bZ[s][:, :], 0.0, slab[s][:, :], ALU.max, ALU.add
                                       ).then_inc(m_h0, 1)
                dve.wait_ge(m_rows, m + 1)
                above(dve, m_rows_stored[s], r * 16)
                v.tensor_copy(natB[s][:, :, :].rearrange("p b d -> p (b d)"), (bXT, bX2)[s][:, :]
                              ).then_inc(m_rows_copied, 1)

            slabs(dve, middle)
            v.memset(numT[:, :], 0.0).then_inc(m_zero, 1)
            dve.wait_ge(m_zero, 1)
            either(L2)

            order = Steps(dve, e_dve)

            def y_sum(m, s, r):
                dve.wait_ge(e_in[s], (r + 1) * 16)
                dve.wait_ge(e_ht, m + 1)
                above(dve, e_rows, m - 1)
                v.scalar_tensor_tensor(zs[s][:, :], slab[s][:, :], 2.0, bZ[s][:, :], ALU.mult, ALU.add
                                       ).then_inc(e_y, 1)

            def moments(m, s):
                order.base, order.k = m * END_STEPS, 0
                dve.wait_ge(e_rows, m + 1)
                for b in range(TG):
                    last = v.bn_stats(stats[:, b, :], bAG[s][:, b * P:b * P + P])
                order(last)
                dve.sem_inc(dve_passed, 1)
                for b in range(TG):
                    last = v.bn_aggr(mv[:, b, :], stats[:, b, :])
                order(last)
                v.tensor_scalar(std[:, :], mv[:, :, 1], EPS, None, ALU.add).then_inc(e_var, 1)
                above(dve, e_out, m)
                dve.wait_ge(e_std, m + 1)
                order(v.reciprocal(rstd[:, :], std[:, :]))
                v.scalar_tensor_tensor(shift[:, :], mv[:, :, 0], -1.0, rstd[:, :], ALU.mult, ALU.mult
                                       ).then_inc(e_norm, 1)

            def end(m, s, r):
                y_sum(m, s, r)
                if not isinstance(m, int) or m >= 1:
                    moments(m - 1, 1 - s)

            slabs(dve, end)
            moments(NS - 1, (NS - 1) % 2)


END_STEPS = 3
STEPS = {True: 22, False: 42}


def kernel(**inputs):
    import numpy as np
    import concourse.bacc as bacc
    from concourse import mybir as _mybir
    from concourse.bass_utils import run_bass_kernel_spmd as run

    x = np.asarray(inputs["x"])
    src = np.asarray(inputs["src"])
    dst = np.asarray(inputs["dst"])
    edges = np.asarray(inputs["edge_attr_128"])
    ep = NT * P
    srcp = np.concatenate([src, np.zeros(ep - E, src.dtype)])
    dstp = np.concatenate([dst, np.full(ep - E, N, dst.dtype)])
    edgep = np.concatenate([edges, np.zeros((ep - E, D), edges.dtype)])
    xp = np.concatenate([x, np.zeros((NP - N, D), x.dtype)])
    t = np.ascontiguousarray
    arrays = {
        "eT": t(edgep.reshape(NG, W, D).transpose(0, 2, 1)),
        "xT": t(xp.T),
        "xrows": t(x),
        "idxT": t(srcp.reshape(NT, P).T),
        "dstT": t(dstp.reshape(NT, P).T),
        "dstR": t(dstp.reshape(CH, TC, P).transpose(1, 0, 2)),
        "dst8": t(dstp.reshape(NT // 8, 8, P)),
        "ends": t(dstp.reshape(NT, P)[:, [0, P - 1]].T),
    }
    for layer in ("1", "2"):
        for w in ("fij", "ni", "nj", "node"):
            arrays[f"w_{w}{layer}"] = t(np.asarray(inputs[f"L0_gnn_W{layer}_{w}"]).T)
        arrays[f"attn{layer}"] = t(np.asarray(inputs[f"L0_gnn_attn{layer}"]).reshape(D, 1))
    nc = bacc.Bacc("TRN2", target_bir_lowering=False, num_devices=1)
    args = {n: nc.dram_tensor(n, a.shape, _mybir.dt.from_np(a.dtype), kind="ExternalInput").ap()
            for n, a in arrays.items()}
    out = nc.dram_tensor("out", (N, D), _mybir.dt.from_np(x.dtype), kind="ExternalOutput").ap()
    program(nc, out=out, **args)
    r = run(nc, [arrays], core_ids=[0])
    return r.results[0]["out"]
```

```python
import concourse.bass as bass
from concourse import mybir
from contextlib import ExitStack

N, E, D = 6250, 106250, 128
P = 128
TG = 4
GC = 8
GS = 4
WIN = 64
TC = TG * GC
W = TG * P
CH = -(-E // (TC * P))
NT = CH * TC
NG = CH * GC
NS = -(-(N + P) // W)
NP = NS * W
XB = 3
BIG = 1e38
SLOPE = 0.2
EPS = 1e-5
SORTED = "dst lies in [0, N], its padding at N"


class Layer:

    def __init__(self, sem, gathered, n, edges_in, proj_hl, proj_m, table, h1_out):
        self.n = n
        self.edges_in, self.proj_hl, self.proj_m = edges_in, proj_hl, proj_m
        self.table, self.h1_out = table, h1_out
        self.loaded = [sem(f"loaded{n}_{g}") for g in range(GS)]
        self.gathered = gathered
        self.uses_before = [(n - 1) * ((CH + XB - 1 - b) // XB) for b in range(XB)]
        self.idx_ready = sem(f"idx_ready{n}")
        self.xt_made = sem(f"xt_made{n}")
        self.xt_copied = sem(f"xt_copied{n}")
        self.onehot_made = sem(f"onehot_made{n}")
        self.z_made = sem(f"z_made{n}")
        self.z_copied = sem(f"z_copied{n}")
        self.f_made = sem(f"f_made{n}")
        self.score_made = sem(f"score_made{n}")
        self.score_copied = sem(f"score_copied{n}")
        self.h1_made = sem(f"h1_made{n}")
        self.h1_stored = [sem(f"h1_stored{n}_{g}") for g in range(GS)] if h1_out is not None else None
        self.soft_pe = sem(f"soft_pe{n}")
        self.soft_dve = sem(f"soft_dve{n}")
        self.soft_act = sem(f"soft_act{n}")
        self.a_made = sem(f"a_made{n}")
        self.num_made = sem(f"num_made{n}")
        self.num_added = sem(f"num_added{n}")
        self.dve_step = sem(f"dve_step{n}")


class Parts:

    def __init__(self, sem, name):
        self.high = sem(f"{name}_high")
        self.rest = sem(f"{name}_rest")
        self.middle = sem(f"{name}_middle")
        self.low = sem(f"{name}_low")
        self.stored = [sem(f"{name}_stored{q}") for q in range(4)]


class Steps:

    def __init__(self, eng, sem):
        self.eng, self.sem, self.base, self.k = eng, sem, 0, 0

    def __call__(self, ins):
        self.k += 1
        ins.then_inc(self.sem, 1)
        self.eng.wait_ge(self.sem, self.base + self.k)


def above(eng, sem, value):
    if not isinstance(value, int) or value > 0:
        eng.wait_ge(sem, value)


def program(nc, eT, xT, xrows, idxT, dstT, dstR, dst8, ends, w_fij1, w_ni1, w_nj1, w_node1, attn1,
            w_fij2, w_ni2, w_nj2, w_node2, attn2, out):
    f32, bf16, i32 = mybir.dt.float32, mybir.dt.bfloat16, mybir.dt.int32
    ALU, ACT = mybir.AluOpType, mybir.ActivationFunctionType
    PE_, DVE_, SP_ = mybir.EngineType.PE, mybir.EngineType.DVE, mybir.EngineType.SP

    projHL = [nc.dram_tensor(f"projHL{n}", [NP, 2 * D], bf16, kind="Internal").ap() for n in (1, 2)]
    projM = [nc.dram_tensor(f"projM{n}", [NP, D], bf16, kind="Internal").ap() for n in (1, 2)]
    h0rows = nc.dram_tensor("h0rows", [NP, D], f32, kind="Internal").ap()
    h1T = nc.dram_tensor("h1T", [NG, P, W], f32, kind="Internal").ap()
    relrow = nc.dram_tensor("relrow", [NG, W], bf16, kind="Internal").ap()
    relrow_g = nc.dram_tensor("relrow_g", [NG, W], bf16, kind="Internal").ap()

    ctx = ExitStack()
    with ctx:
        def sb(name, shape, dt=f32):
            return ctx.enter_context(nc.sbuf_tensor(name, shape, dt))

        def pb(name):
            return ctx.enter_context(nc.psum_tensor(name, [P, W], f32))

        def sem(name):
            return ctx.enter_context(nc.semaphore(name))

        ident = sb("ident", [P, P])
        iota_row = sb("iota_row", [P, P])
        iota_col = sb("iota_col", [P, 1])
        iota_win = sb("iota_win", [P, 1])
        win_off = sb("win_off", [P, 1])
        ones = sb("ones", [P, P])
        wts = sb("wts", [P, 8, P])
        attn = sb("attn", [P, 2])
        attn_at = sb("attn_at", [P, 2, 2 * TC - 1])
        FIJ, NI, NJ, NODE = 0, 1, 2, 3

        idx_all = sb("idx_all", [P, NT], i32)
        dst_rows = sb("dst_rows", [TC, CH, P], i32)
        dst_col = sb("dst_col", [P, NT], i32)
        rel_col = sb("rel_col", [P, NT])
        base_all = sb("base_all", [P, NT], i32)
        fits = sb("fits", [1, 4], i32)
        span = sb("span", [1, NG])
        widest = sb("widest", [1, 1])
        base_row = sb("base_row", [1, NT], i32)
        last_row = sb("last_row", [1, NT], i32)
        group_row = sb("group_row", [1, NG], i32)
        cont = sb("cont", [1, NT + 1])
        whole = sb("whole", [1, NT + 1])
        keepA = sb("keepA", [1, NT + 1])
        keepE = sb("keepE", [1, NT + 1])
        penC = sb("penC", [1, NT + 1])
        penA = sb("penA", [1, NT + 1])
        penE = sb("penE", [1, NT + 1])
        dst8_t = sb("dst8_t", [NT // 8, 8, P], i32)
        rel8 = sb("rel8", [NT // 8, 8, P], bf16)
        rel8g = sb("rel8g", [NT // 8, 2, W], bf16)

        edge_in = [sb(f"edge_in{g}", [P, W]) for g in range(GS)]
        window = [sb(f"window{g}", [P, 3 * TG, P], bf16) for g in range(GS)]
        rel_bc = [sb(f"rel_bc{g}", [P, W], bf16) for g in range(GS)]
        xsrc = [sb(f"xsrc{b}", [P, TC, P]) for b in range(XB)]
        idx_slot = [sb(f"idx_slot{b}", [P, TC], i32) for b in range(XB)]
        xsT = [sb(f"xsT{s}", [P, W]) for s in range(2)]
        onehot = [sb(f"onehot{s}", [P, W], bf16) for s in range(2)]
        zc = [sb(f"zc{s}", [P, W]) for s in range(2)]
        h1 = [sb(f"h1_{s}", [P, W]) for s in range(GS)]
        fT = [sb(f"fT{s}", [P, W]) for s in range(2)]
        amat = [sb(f"amat{s}", [P, TG, P]) for s in range(2)]
        apair = [a[:, :, :].rearrange("p i (h j) -> p (i h) j", j=WIN) for a in amat]
        numT = sb("numT", [P, NP])

        score_sb = sb("score_sb", [TC, P])
        keep = sb("keep", [TC, P + 1])
        pen = sb("pen", [TC, P + 1])
        isF = sb("isF", [TC, P])
        isL = sb("isL", [TC, P])
        penF = sb("penF", [TC, P])
        penL = sb("penL", [TC, P])
        scanF = sb("scanF", [TC, P])
        scanB = sb("scanB", [TC, P])
        seg = sb("seg", [TC, P])
        aexp = sb("aexp", [TC, P])
        cd = sb("cd", [TC, 2])
        rowC = sb("rowC", [1, TC + 1])
        rowD = sb("rowD", [1, TC])
        sumC = sb("sumC", [1, TC + 1])
        sumD = sb("sumD", [1, TC])
        u1 = sb("u1", [1, TC])
        u2 = sb("u2", [1, TC])
        u3 = sb("u3", [1, TC])
        ecar = sb("ecar", [1, 2])
        cfac = sb("cfac", [1, 1])
        rcol = sb("rcol", [P, TC])
        wcol = sb("wcol", [P, TC + 1])
        relc = sb("relc", [P, TC])

        zs = h1[0:2]
        slab = [xsrc[2][:, q * TG:(q + 1) * TG, :].rearrange("p b d -> p (b d)") for q in range(4)]
        part_hl = [xsrc[2][:, (4 + q) * TG:(5 + q) * TG, :].rearrange("p b d -> p (b d)").bitcast(bf16)
                   .rearrange("p (b h d) -> p b h d", h=2, d=P) for q in range(4)]
        part_m = [h1[2 + q // 2][:, q % 2 * (W // 2):(q % 2 + 1) * (W // 2)].bitcast(bf16)
                  .rearrange("p (b d) -> p b d", d=P) for q in range(4)]
        rest = amat
        node_rows = [xsrc[1][:, q * TG:(q + 1) * TG, :] for q in range(4)]
        stats = sb("stats", [P, TG, 6])
        mv = sb("mv", [P, TG, 2])
        std = sb("std", [P, TG])
        rstd = sb("rstd", [P, TG])
        shift = sb("shift", [P, TG])

        bXT, bX2, bSC, bSM = pb("bXT"), pb("bX2"), pb("bSC"), pb("bSM")
        bZ = [pb("bZ0"), pb("bZ1")]
        bAG = [pb("bAG0"), pb("bAG1")]
        END_F, END_B = bSM[0:1, 128:128 + TC], bSM[0:1, 160:160 + TC]
        CD = bSM[0:TC, 192:194]
        SEND_F, SEND_B = bSM[0:1, 224:224 + TC], bSM[0:1, 256:256 + TC]
        SCD = bSM[0:TC, 288:290]
        ACOL, TCOL, CCOL = bSM[:, 320:320 + TC], bSM[:, 352:352 + TC], bSM[:, 384:385]

        pe_passed, dve_passed, pool_passed = sem("pe_passed"), sem("dve_passed"), sem("pool_passed")
        const_in = sem("const_in")
        idx_in = sem("idx_in")
        graph_in = sem("graph_in")
        rel8_in = sem("rel8_in")
        const_made = sem("const_made")
        iota_made = sem("iota_made")
        rel8_made = sem("rel8_made")
        rel_stored = sem("rel_stored")
        fits_made = sem("fits_made")
        attn_made = sem("attn_made")
        rel_made = sem("rel_made")
        dve_pro = sem("dve_pro")
        gathered = [[sem(f"gathered{b}_{g}") for g in range(GC)] for b in range(XB)]
        L1 = Layer(sem, gathered, 1, eT, projHL[0], projM[0], xrows, h1T)
        L2 = Layer(sem, gathered, 2, h1T, projHL[1], projM[1], h0rows, None)
        four = lambda name: [sem(f"{name}{q}") for q in range(4)]
        p_in, m_in, e_in = four("p_in"), four("m_in"), four("e_in")
        p_made = sem("p_made")
        p_parts = Parts(sem, "p")
        m_ht = sem("m_ht")
        m_h0 = sem("m_h0")
        m_zero = sem("m_zero")
        m_proj = sem("m_proj")
        m_parts = Parts(sem, "m")
        m_rows = sem("m_rows")
        m_rows_copied = sem("m_rows_copied")
        m_rows_stored = four("m_rows_stored")
        e_ht = sem("e_ht")
        e_y = sem("e_y")
        e_rows = sem("e_rows")
        e_var = sem("e_var")
        e_std = sem("e_std")
        e_norm = sem("e_norm")
        e_out = sem("e_out")
        e_dve = sem("e_dve")
        e_stored = four("e_stored")

        block = ctx.enter_context(nc.Block())
        consts = [w_fij1, w_ni1, w_nj1, w_node1, w_fij2, w_ni2, w_nj2, w_node2]
        rows4 = lambda t, m: t[bass.ds(m * W, W), :].rearrange("(b p) d -> p b d", p=P)
        slot_uses = [(NS + 3 - q) // 4 for q in range(4)]

        def slabs(eng, body):
            for m in range(4):
                body(m, m % 2, m, 0)
            turns = NS // 4 - 1
            with eng.Fori(0, turns) as j:
                for q in range(4):
                    body(j * 4 + (4 + q), q % 2, q, j + 1)
            for m in range(4 + 4 * turns, NS):
                body(m, m % 2, m % 4, m // 4)

        def reached(m, first):
            return not isinstance(m, int) or m >= first

        def back(m, q, t, by):
            return m - by, (q - by) % 2, (q - by) % 4, t if q >= by else t - 1

        def act_parts(act, made, parts, table_hl, table_m, m, q, t, lag):
            if reached(m, lag) and not (isinstance(m, int) and m >= NS + lag):
                k, s, u, w = back(m, q, t, lag)
                act.wait_ge(made, k + 1)
                above(act, parts.stored[u], w * 32)
                nc.scalar.copy(part_hl[u][:, :, 0, :], bAG[s][:, :].rearrange("p (b d) -> p b d", d=P)
                               ).then_inc(parts.high, 1)
            if reached(m, lag + 1) and not (isinstance(m, int) and m >= NS + lag + 1):
                k, s, u, w = back(m, q, t, lag + 1)
                act.wait_ge(parts.rest, k + 1)
                nc.scalar.copy(part_m[u], rest[s][:, :, :]).then_inc(parts.middle, 1)
            if reached(m, lag + 2):
                k, s, u, w = back(m, q, t, lag + 2)
                act.wait_ge(parts.low, k + 1)
                act.dma_start(rows4(table_hl, k), part_hl[u].rearrange("p b h d -> p b (h d)")
                              ).then_inc(parts.stored[u], 16)
                act.dma_start(rows4(table_m, k), part_m[u]).then_inc(parts.stored[u], 16)

        def dve_parts(dve, parts, m, q, t, lag):
            if reached(m, lag) and not (isinstance(m, int) and m >= NS + lag):
                k, s, u, w = back(m, q, t, lag)
                above(dve, parts.low, k - 1)
                dve.wait_ge(parts.high, k + 1)
                nc.vector.tensor_tensor(rest[s][:, :, :], bAG[s][:, :].rearrange("p (b d) -> p b d", d=P),
                                        part_hl[u][:, :, 0, :], ALU.subtract).then_inc(parts.rest, 1)
            if reached(m, lag + 1):
                k, s, u, w = back(m, q, t, lag + 1)
                dve.wait_ge(parts.middle, k + 1)
                nc.vector.tensor_tensor(part_hl[u][:, :, 1, :], rest[s][:, :, :], part_m[u], ALU.subtract
                                        ).then_inc(parts.low, 1)

        @block.sync
        def _(sp):
            sp.dma_start(dst8_t[:, :, :], dst8).then_inc(rel8_in, 16)
            sp.dma_start(base_all[:, :], ends[0:1, :].partition_broadcast(P)).then_inc(graph_in, 16)
            sp.dma_start(dst_col[:, :], dstT).then_inc(graph_in, 16)
            sp.dma_start(base_row[:, :], ends[0:1, :]).then_inc(graph_in, 16)
            sp.dma_start(last_row[:, :], ends[1:2, :]).then_inc(graph_in, 16)
            sp.dma_start(dst_rows[:, :, :], dstR).then_inc(graph_in, 16)

            def slab_in(arrived, used):
                def body(m, s, q, t):
                    above(sp, used, m - 3)
                    sp.dma_start(slab[q], xT[:, bass.ds(m * W, W)]).then_inc(arrived[q], 16)
                return body

            slabs(sp, slab_in(p_in, p_made))

            sp.wait_ge(rel8_made, 1)
            sp.dma_start(relrow.rearrange("(p a) w -> p (a w)", a=2),
                         rel8[:, :, :].rearrange("p a e -> p (a e)")).then_inc(rel_stored, 16)
            sp.dma_start(relrow_g.rearrange("(p a) w -> p (a w)", a=2),
                         rel8g[:, :, :].rearrange("p a e -> p (a e)")).then_inc(rel_stored, 16)
            sp.wait_ge(rel_stored, 32)

            def load_layer(L, narrow):
                def first_nodes(row, at, count):
                    _, first = nc.values_load_multi_w_load_instructions(
                        row[0:1, bass.ds(at, count)], engines=(SP_,), min_val=0, max_val=N,
                        skip_runtime_bounds_check_because=SORTED)
                    return first

                def chunk(c):
                    if narrow:
                        first = first_nodes(group_row, c * GC, GC)
                    for g in range(GC):
                        n, q = c * GC + g, g % GS
                        above(sp, L.z_made, n - (GS - 1))
                        if L.h1_out is not None:
                            above(sp, L.h1_made, n - (GS - 1))
                        sp.dma_start(edge_in[q][:, :], L.edges_in[bass.ds(n, 1), :, :].rearrange(
                            "o p w -> (o p) w")).then_inc(L.loaded[q], 16)
                        if narrow:
                            sp.dma_start(rel_bc[q][:, :], relrow_g[bass.ds(n, 1), :].partition_broadcast(P)
                                         ).then_inc(L.loaded[q], 16)
                            sp.dma_start(window[q][0:WIN, 0:2, :].rearrange("p h d -> p (h d)"),
                                         L.proj_hl[bass.ds(first[g], WIN), :]).then_inc(L.loaded[q], 16)
                            sp.dma_start(window[q][WIN:2 * WIN, 0, :], L.proj_m[bass.ds(first[g], WIN), :]
                                         ).then_inc(L.loaded[q], 16)
                        else:
                            first = first_nodes(base_row, n * TG, TG)
                            sp.dma_start(rel_bc[q][:, :], relrow[bass.ds(n, 1), :].partition_broadcast(P)
                                         ).then_inc(L.loaded[q], 16)
                            for i in range(TG):
                                sp.dma_start(window[q][:, 3 * i:3 * i + 2, :].rearrange("p h d -> p (h d)"),
                                             L.proj_hl[bass.ds(first[i], P), :]).then_inc(L.loaded[q], 16)
                                sp.dma_start(window[q][:, 3 * i + 2, :], L.proj_m[bass.ds(first[i], P), :]
                                             ).then_inc(L.loaded[q], 16)
                        if L.h1_out is not None and not (isinstance(c, int) and n < GS):
                            store_h1(L, n - GS, q)
                return chunk

            def store_h1(L, n, q):
                sp.wait_ge(L.h1_made, n + 1)
                sp.dma_start(L.h1_out[bass.ds(n, 1), :, :].rearrange("o p w -> (o p) w"), h1[q][:, :]
                             ).then_inc(L.h1_stored[q], 16)

            def layer(L, narrow):
                chunk = load_layer(L, narrow)
                chunk(0)
                with sp.Fori(1, CH) as c:
                    chunk(c)
                if L.h1_out is not None:
                    for n in range(NG - GS, NG):
                        store_h1(L, n, n % GS)
                    for q in range(GS):
                        sp.wait_ge(L.h1_stored[q], 16 * (NG // GS))

            sp.wait_ge(fits_made, 1)
            fit = nc.sync.value_load(fits[0:1, 0:1], min_val=0, max_val=1)

            def either(L):
                with sp.If(fit == 1):
                    layer(L, True)
                with sp.Else():
                    layer(L, False)

            for q in range(4):
                sp.wait_ge(p_parts.stored[q], 32 * slot_uses[q])
            sp.wait_ge(graph_in, 16 * 5)
            either(L1)

            def rows_out(table, copied, stored, m, q):
                sp.wait_ge(copied, m + 1)
                sp.dma_start(rows4(table, m), node_rows[q]).then_inc(stored[q], 16)

            slab_m = slab_in(m_in, m_h0)

            def middle(m, s, q, t):
                slab_m(m, s, q, t)
                if reached(m, 2):
                    rows_out(h0rows, m_rows_copied, m_rows_stored, m - 2, (q - 2) % 4)

            sp.wait_ge(L1.num_made, CH // XB * XB * GC)
            slabs(sp, middle)
            for m in (NS - 2, NS - 1):
                rows_out(h0rows, m_rows_copied, m_rows_stored, m, m % 4)
            for q in range(4):
                sp.wait_ge(m_rows_stored[q], 16 * slot_uses[q])
                sp.wait_ge(m_parts.stored[q], 32 * slot_uses[q])
            either(L2)

            slab_e = slab_in(e_in, e_y)

            def end(m, s, q, t):
                slab_e(m, s, q, t)
                if reached(m, 2):
                    rows_out(out, e_out, e_stored, m - 2, (q - 2) % 4)

            sp.wait_ge(L2.num_made, CH // XB * XB * GC)
            slabs(sp, end)
            rows_out(out, e_out, e_stored, NS - 2, (NS - 2) % 4)
            m, q = NS - 1, (NS - 1) % 4
            sp.wait_ge(e_out, m + 1)
            sp.dma_start(out[m * W:N, :], node_rows[q][0:N - m * W, 0, :]).then_inc(e_stored[q], 16)
            for q in range(4):
                sp.wait_ge(e_stored[q], 16 * slot_uses[q])

        @block.gpsimd
        def _(pool):
            pool.dma_start(idx_all[:, :], idxT).then_inc(idx_in, 16)
            nc.gpsimd.iota(iota_row[:, :], [[1, P]], base=0, channel_multiplier=0,
                           allow_small_or_imprecise_dtypes=True).then_inc(iota_made, 1)
            nc.gpsimd.iota(iota_col[:, :], [[0, 1]], base=0, channel_multiplier=1,
                           allow_small_or_imprecise_dtypes=True).then_inc(iota_made, 1)
            nc.gpsimd.memset(ones[:, :], 1.0).then_inc(iota_made, 1)
            pool.wait_ge(iota_made, 3)
            nc.gpsimd.affine_select(out=ident[:, :], in_=ones[:, :], compare_op=ALU.is_equal, fill=0.0,
                                    base=0, pattern=[[-1, P]], channel_multiplier=1).then_inc(const_made, 1)
            pool.wait_ge(idx_in, 16)

            def layer(L):
                def chunk(c, b, again):
                    if again:
                        pool.wait_ge(L.num_made, (c - XB) * GC + 1)
                    nc.gpsimd.tensor_copy(idx_slot[b][:, :], idx_all[:, bass.ds(c * TC, TC)]
                                          ).then_inc(L.idx_ready, 1)
                    pool.wait_ge(L.idx_ready, c + 1)
                    pool.sem_inc(pool_passed, 1)
                    for g in range(GC):
                        if again:
                            pool.wait_ge(L.num_made, (c - XB) * GC + g + 1)
                            pool.sem_inc(pool_passed, 1)
                        for i in range(g * TG, g * TG + TG):
                            pool.indirect_dma_start(
                                xsrc[b][:, i, :], None, L.table,
                                bass.IndirectOffsetOnAxis(ap=idx_slot[b][:, i:i + 1], axis=0)
                            ).then_inc(L.gathered[b][g], 16)

                for c in range(XB):
                    if L.n == 1 and c == 2:
                        pool.wait_ge(p_made, NS)
                        for q in range(4):
                            pool.wait_ge(p_parts.stored[q], 32 * slot_uses[q])
                    chunk(c, c, False)
                turns = (CH - XB) // XB
                with pool.Fori(0, turns) as j:
                    for b in range(XB):
                        chunk(j * XB + (XB + b), b, True)
                for c in range(XB + turns * XB, CH):
                    chunk(c, c % XB, True)

            layer(L1)
            for q in range(4):
                pool.wait_ge(m_rows_stored[q], 16 * slot_uses[q])
                pool.wait_ge(m_parts.stored[q], 32 * slot_uses[q])
            layer(L2)

        @block.scalar
        def _(act):
            for k, w in enumerate(consts):
                act.dma_start(wts[:, k, :], w).then_inc(const_in, 16)
            act.dma_start(attn[:, 0:1], attn1).then_inc(const_in, 16)
            act.dma_start(attn[:, 1:2], attn2).then_inc(const_in, 16)

            def project(m, s, q, t):
                act_parts(act, p_made, p_parts, projHL[0], projM[0], m, q, t, 0)

            slabs(act, project)
            for m in (NS, NS + 1):
                project(m, m % 2, m % 4, m // 4)

            def layer(L):
                def slot(c, g, front, soft):
                    n, s = c * GC + g, g % 2
                    if soft and g == 3:
                        act.wait_ge(L.soft_dve, (c - 1) * 6 + 3)
                        nc.scalar.activation(aexp[:, :], seg[:, :], ACT.Exp)
                        nc.scalar.activation(ecar[0:1, 1:2], ecar[0:1, 0:1], ACT.Exp).then_inc(L.soft_act, 1)
                    if front:
                        act.wait_ge(L.z_made, n + 1)
                        above(act, L.f_made, n - 1)
                        if L.h1_out is not None:
                            above(act, L.h1_made, n - 1)
                        nc.scalar.copy(zc[s][:, :], bZ[s][:, :]).then_inc(L.z_copied, 1)
                    if g == 0 and soft:
                        act.wait_ge(L.score_made, c * GC)
                        above(act, L.soft_dve, (c - 1) * 6 - 3)
                        nc.scalar.copy(score_sb[:, :], bSC[0:TC, 0:P]).then_inc(L.score_copied, 1)
                    if front and not (isinstance(c, int) and n == NG - 1):
                        copy_rows(n + 1, 1 - s)

                def copy_rows(n, s):
                    act.wait_ge(L.xt_made, n + 1)
                    above(act, L.z_made, n - 1)
                    nc.scalar.copy(xsT[s][:, :], bXT[:, :]).then_inc(L.xt_copied, 1)

                def turn(c, front, soft):
                    for g in range(GC):
                        slot(c, g, front, soft)

                copy_rows(0, 0)
                turn(0, True, False)
                turn(1, True, True)
                with act.Fori(2, CH - 1) as c:
                    turn(c, True, True)
                turn(CH - 1, True, True)
                turn(CH, False, True)

            layer(L1)

            def middle(m, s, q, t):
                act_parts(act, m_proj, m_parts, projHL[1], projM[1], m, q, t, 1)
                if reached(m, 1) and not (isinstance(m, int) and m > NS):
                    k, s, u, w = back(m, q, t, 1)
                    act.wait_ge(m_rows, k + 1)
                    above(act, m_rows_stored[u], w * 16)
                    nc.scalar.copy(node_rows[u].rearrange("p b d -> p (b d)"), (bXT, bX2)[s][:, :]
                                   ).then_inc(m_rows_copied, 1)

            slabs(act, middle)
            for m in range(NS, NS + 3):
                middle(m, m % 2, m % 4, m // 4)
            layer(L2)

            def end(m, s, q, t):
                act.wait_ge(e_var, m + 1)
                nc.scalar.activation(std[:, :], std[:, :], ACT.Sqrt).then_inc(e_std, 1)
                act.wait_ge(e_norm, m + 1)
                above(act, e_stored[q], t * 16)
                for b in range(TG):
                    last = nc.scalar.activation(node_rows[q][:, b, :], bAG[s][:, b * P:b * P + P], ACT.Identity,
                                                bias=shift[:, b:b + 1], scale=rstd[:, b:b + 1])
                last.then_inc(e_out, 1)

            slabs(act, end)

        @block.tensor
        def _(pe):
            mm, tp = nc.tensor.matmul, nc.tensor.transpose
            pe.wait_ge(const_made, 1)
            pe.wait_ge(const_in, 16 * 10)

            def project(m, s, q, t):
                pe.wait_ge(p_in[q], (t + 1) * 16)
                above(pe, p_parts.rest, m - 1)
                for b in range(TG):
                    last = mm(bAG[s][:, b * P:b * P + P], slab[q][:, b * P:b * P + P], wts[:, NJ, :],
                              start=True, stop=True)
                last.then_inc(p_made, 1)

            slabs(pe, project)

            def layer(L, narrow):
                ready = 64 if narrow else 160
                fij, ni = wts[:, (L.n - 1) * 4 + FIJ, :], wts[:, (L.n - 1) * 4 + NI, :]

                def transposed_rows(c, g, b, rounds):
                    n, s = c * GC + g, g % 2
                    uses = rounds + (L.uses_before[b] + 1)
                    pe.wait_ge(L.gathered[b][g], uses * (16 * TG))
                    above(pe, L.xt_copied, n)
                    for i in range(TG):
                        last = tp(bXT[:, i * P:i * P + P], xsrc[b][:, g * TG + i, :], ident[:, :])
                    last.then_inc(L.xt_made, 1)

                def z_sum(c, g):
                    n, s, q = c * GC + g, g % 2, g % GS
                    above(pe, L.z_copied, n - 1)
                    pe.wait_ge(L.loaded[q], (c * (GC // GS) + g // GS + 1) * ready)
                    mm(bZ[s][:, :], fij, edge_in[q][:, :], start=True, stop=False)
                    pe.wait_ge(L.onehot_made, n + 1)
                    if narrow:
                        mm(bZ[s][:, :], window[q][:, 0, :], onehot[s][:, :], start=False, stop=False)
                        mm(bZ[s][:, :], window[q][0:WIN, 1, :], onehot[s][0:WIN, :], start=False, stop=False)
                    else:
                        for i in range(TG):
                            for part in range(3):
                                mm(bZ[s][:, i * P:i * P + P], window[q][:, 3 * i + part, :],
                                   onehot[s][:, i * P:i * P + P], start=False, stop=False, skip_group_check=True)
                    pe.wait_ge(L.xt_copied, n + 1)
                    last = mm(bZ[s][:, :], ni, xsT[s][:, :], start=False, stop=True)
                    last.then_inc(L.z_made, 1)

                def scores(c, g):
                    n, s = c * GC + g, g % 2
                    pe.wait_ge(L.f_made, n + 1)
                    if g == 0:
                        above(pe, L.score_copied, c)
                    for i in range(TG):
                        t = g * TG + i
                        last = mm(bSC[0:TC, 0:P], attn_at[:, L.n - 1, TC - 1 - t:2 * TC - 1 - t],
                                  fT[s][:, i * P:i * P + P], start=t == 0, stop=t == TC - 1)
                    last.then_inc(L.score_made, 1)

                def partial(k, g, b):
                    n, s = k * GC + g, g % 2
                    if narrow:
                        pe.wait_ge(L.a_made, k * (GC // 2) + g // 2 + 1)
                    else:
                        pe.wait_ge(L.a_made, n + 1)
                    above(pe, L.num_added, n - 1)
                    for i in range(TG):
                        rows = xsrc[b][:, g * TG + i, :]
                        if narrow:
                            last = mm(bAG[s][:, 0:WIN], rows, apair[g // 2 % 2][:, g % 2 * TG + i, :],
                                      start=i == 0, stop=i == TG - 1)
                        else:
                            last = mm(bAG[s][:, i * P:i * P + P], rows, amat[s][:, i, :], start=True, stop=True)
                    last.then_inc(L.num_made, 1)

                def ends_to_row(k, step, f, b):
                    pe.wait_ge(L.soft_dve, k * 6 + step)
                    pe.sem_inc(pe_passed, 1)
                    tp(f, scanF[:, P - 1:P], ident[0:TC, 0:TC])
                    tp(b, scanB[:, 0:1], ident[0:TC, 0:TC]).then_inc(L.soft_pe, 1)

                def row_to_cols(k, step, cols, c_row, d_row):
                    pe.wait_ge(L.soft_dve, k * 6 + step)
                    pe.sem_inc(pe_passed, 1)
                    tp(cols[:, 0:1], c_row[0:1, 0:TC], ident[0:1, 0:1])
                    tp(cols[:, 1:2], d_row[0:1, 0:TC], ident[0:1, 0:1]).then_inc(L.soft_pe, 1)

                def weights_to_cols(k):
                    pe.wait_ge(L.soft_dve, k * 6 + 6)
                    pe.sem_inc(pe_passed, 1)
                    tp(ACOL, aexp[:, :], ident[0:TC, 0:TC])
                    tp(TCOL, seg[:, :], ident[0:TC, 0:TC])
                    mm(CCOL, ones[0:1, :], cfac[0:1, 0:1], start=True, stop=True).then_inc(L.soft_pe, 1)

                def turn(c, b, rounds, has_front, soft, agg, has_next=True):
                    for g in range(GC):
                        if has_front:
                            z_sum(c, g)
                        if g == 0:
                            if soft:
                                scores(c - 1, GC - 1)
                        elif has_front:
                            scores(c, g - 1)
                        if has_front and g < GC - 1:
                            transposed_rows(c, g + 1, b, rounds)
                        elif has_front and has_next:
                            transposed_rows(c + 1, 0, (b + 1) % XB, rounds + (b + 1) // XB)
                        if agg:
                            partial(c - 2, g, (b - 2) % XB)
                        if soft:
                            if g == 1:
                                ends_to_row(c - 1, 1, END_F, END_B)
                            if g == 2:
                                row_to_cols(c - 1, 2, CD, rowC, rowD)
                            if g == 4:
                                ends_to_row(c - 1, 4, SEND_F, SEND_B)
                            if g == 5:
                                row_to_cols(c - 1, 5, SCD, sumC, sumD)
                            if g == 6:
                                weights_to_cols(c - 1)

                transposed_rows(0, 0, 0, 0)
                for c in range(XB):
                    turn(c, c, 0, True, c >= 1, c >= 2)
                turns = (CH - XB) // XB
                with pe.Fori(0, turns) as j:
                    for b in range(XB):
                        turn(j * XB + (XB + b), b, j + 1, True, True, True)
                for c in range(XB + turns * XB, CH + 2):
                    turn(c, c % XB, c // XB, c < CH, c <= CH, True, c < CH - 1)

            pe.wait_ge(attn_made, 2)
            pe.wait_ge(fits_made, 1)
            fit = nc.tensor.value_load(fits[0:1, 0:1], min_val=0, max_val=1)

            def either(L):
                with pe.If(fit == 1):
                    layer(L, True)
                with pe.Else():
                    layer(L, False)

            either(L1)

            def node_sum(made, used, node, m, s):
                above(pe, used, m - 1)
                mm(bZ[s][:, :], node, numT[:, bass.ds(m * W, W)], start=True, stop=True).then_inc(made, 1)

            def middle_rest(m, s):
                pe.wait_ge(m_h0, m + 1)
                above(pe, m_parts.rest, m - 1)
                for b in range(TG):
                    last = mm(bAG[s][:, b * P:b * P + P], zs[s][:, b * P:b * P + P], wts[:, 4 + NJ, :],
                              start=True, stop=True)
                last.then_inc(m_proj, 1)
                bank = (bXT, bX2)[s]
                above(pe, m_rows_copied, m - 1)
                for b in range(TG):
                    last = tp(bank[:, b * P:b * P + P], zs[s][:, b * P:b * P + P], ident[:, :])
                last.then_inc(m_rows, 1)

            def middle(m, s, q, t):
                node_sum(m_ht, m_h0, wts[:, NODE, :], m, s)
                if not isinstance(m, int) or m >= 1:
                    middle_rest(m - 1, 1 - s)

            pe.wait_ge(L1.num_added, NG)
            slabs(pe, middle)
            middle_rest(NS - 1, (NS - 1) % 2)

            either(L2)

            def end_rest(m, s):
                pe.wait_ge(e_y, m + 1)
                above(pe, e_out, m - 1)
                for b in range(TG):
                    last = tp(bAG[s][:, b * P:b * P + P], zs[s][:, b * P:b * P + P], ident[:, :])
                last.then_inc(e_rows, 1)

            def end(m, s, q, t):
                node_sum(e_ht, e_y, wts[:, 4 + NODE, :], m, s)
                if not isinstance(m, int) or m >= 1:
                    end_rest(m - 1, 1 - s)

            pe.wait_ge(L2.num_added, NG)
            slabs(pe, end)
            end_rest(NS - 1, (NS - 1) % 2)

        @block.vector
        def _(dve):
            v = nc.vector
            step = Steps(dve, dve_pro)
            dve.wait_ge(rel8_in, 16)
            v.tensor_tensor(rel8[:, :, :], dst8_t[:, :, :], dst8_t[:, :, 0:1].broadcast_to((NT // 8, 8, P)),
                            ALU.subtract)
            by_group = dst8_t[:, :, :].rearrange("p (a i) e -> p a (i e)", a=2)
            v.tensor_tensor(rel8g[:, :, :], by_group, by_group[:, :, 0:1].broadcast_to((NT // 8, 2, W)),
                            ALU.subtract).then_inc(rel8_made, 1)
            v.memset(numT[:, :], 0.0)
            v.memset(keep[:, :], 0.0)
            step(v.memset(pen[:, :], 0.0))
            dve.wait_ge(graph_in, 16 * 5)
            v.tensor_copy(group_row[0:1, :], base_row[0:1, ::TG])
            v.memset(fits[:, :], 0)
            step(v.tensor_tensor(span[0:1, :], last_row[0:1, TG - 1::TG], base_row[0:1, ::TG], ALU.subtract))
            step(v.tensor_reduce(widest[0:1, :], span[0:1, :], mybir.AxisListType.X, ALU.max))
            v.tensor_scalar(fits[0:1, 0:1], widest[0:1, :], WIN - 0.5, None, ALU.is_lt).then_inc(fits_made, 1)
            v.memset(cont[:, :], 0.0)
            v.memset(whole[:, :], 0.0)
            v.memset(keepA[:, :], 0.0)
            step(v.memset(keepE[:, :], 0.0))
            v.tensor_tensor(cont[0:1, 1:NT], base_row[0:1, 1:NT], last_row[0:1, 0:NT - 1], ALU.is_equal)
            step(v.tensor_tensor(whole[0:1, 0:NT], base_row[0:1, :], last_row[0:1, :], ALU.is_equal))
            v.tensor_tensor(keepA[0:1, 1:NT + 1], cont[0:1, 1:NT + 1], whole[0:1, 0:NT], ALU.mult)
            step(v.tensor_tensor(keepE[0:1, :], cont[0:1, :], whole[0:1, :], ALU.mult))
            v.tensor_scalar(penC[0:1, :], cont[0:1, :], BIG, -BIG, ALU.mult, ALU.add)
            v.tensor_scalar(penA[0:1, :], keepA[0:1, :], BIG, -BIG, ALU.mult, ALU.add)
            step(v.tensor_scalar(penE[0:1, :], keepE[0:1, :], BIG, -BIG, ALU.mult, ALU.add))
            dve.wait_ge(iota_made, 3)
            step(v.tensor_scalar(win_off[:, :], iota_col[:, :], WIN - 0.5, -float(WIN), ALU.is_gt, ALU.mult))
            step(v.tensor_tensor(iota_win[:, :], iota_col[:, :], win_off[:, :], ALU.add))

            def project(m, s, q, t):
                dve_parts(dve, p_parts, m, q, t, 0)

            slabs(dve, project)
            project(NS, NS % 2, NS % 4, NS // 4)
            dve.wait_ge(const_in, 16 * 10)
            v.memset(attn_at[:, :, :], 0.0).then_inc(attn_made, 1)
            dve.wait_ge(attn_made, 1)
            v.tensor_copy(attn_at[:, :, TC - 1], attn[:, :]).then_inc(attn_made, 1)
            dve.wait_ge(fits_made, 1)
            fit = v.value_load(fits[0:1, 0:1], min_val=0, max_val=1)

            def layer(L, narrow):
                one = L.h1_out is not None
                step = Steps(dve, L.dve_step)
                ready = 64 if narrow else 160

                cols = lambda a: a[:, :].rearrange("p (n i) -> p n i", i=TG if narrow else 1)
                v.tensor_tensor(cols(rel_col), cols(dst_col), cols(base_all)[:, :, 0:1].broadcast_to(
                    tuple(cols(dst_col).shape)), ALU.subtract)
                v.memset(rowC[:, :], -BIG)
                v.memset(sumC[:, :], 0.0)
                v.memset(sumD[:, :], 0.0)
                step(v.memset(rowD[:, :], -BIG))

                def masks(k):
                    d = dst_rows[:, k, :]
                    v.tensor_tensor(keep[:, 1:P], d[:, 1:P], d[:, 0:P - 1], ALU.is_equal)
                    v.tensor_tensor(isF[:, :], d, d[:, 0:1].broadcast_to((TC, P)), ALU.is_equal)
                    step(v.tensor_tensor(isL[:, :], d, d[:, P - 1:P].broadcast_to((TC, P)), ALU.is_equal))
                    v.tensor_scalar(pen[:, 1:P], keep[:, 1:P], BIG, -BIG, ALU.mult, ALU.add)
                    v.tensor_scalar(penF[:, :], isF[:, :], BIG, -BIG, ALU.mult, ALU.add)
                    step(v.tensor_scalar(penL[:, :], isL[:, :], BIG, -BIG, ALU.mult, ALU.add))

                def row_maxima(k):
                    dve.wait_ge(L.score_copied, k + 1)
                    v.tensor_tensor_scan(scanF[:, :], pen[:, 0:P], score_sb[:, :], -BIG, ALU.add, ALU.max)
                    step(v.tensor_tensor_scan(scanB[:, ::-1], pen[:, P:0:-1], score_sb[:, ::-1], -BIG, ALU.add, ALU.max))
                    v.tensor_tensor(seg[:, :], scanF[:, :], scanB[:, :], ALU.max).then_inc(L.soft_dve, 1)

                def chain(k, at, ends_f, ends_b, from_before, row, back, pa, pe_, pc, op0, op1, last):
                    dve.wait_ge(L.soft_pe, k * 5 + at - 1)
                    v.tensor_tensor(u1[0:1, :], ends_f, pc[0:1, bass.ds(k * TC + 1, TC)], op0)
                    if from_before is None:
                        v.tensor_copy(row[0:1, 0:1], row[0:1, TC:TC + 1])
                    else:
                        v.tensor_tensor(row[0:1, 0:1], row[0:1, TC:TC + 1], from_before, ALU.mult)
                    v.tensor_copy(u3[0:1, 0:TC - 1], pe_[0:1, bass.ds(k * TC + 1, TC - 1)])
                    step(v.tensor_tensor(u2[0:1, 0:TC - 1], ends_b[0:1, 1:TC], pc[0:1, bass.ds(k * TC + 1, TC - 1)],
                                         op0))
                    v.tensor_tensor_scan(row[0:1, 1:TC + 1], pa[0:1, bass.ds(k * TC + 1, TC)], u1[0:1, :],
                                         row[0:1, 0:1], op0, op1)
                    v.tensor_tensor_scan(back[0:1, TC - 2::-1], u3[0:1, TC - 2::-1],
                                         u2[0:1, TC - 2::-1], last, op0, op1).then_inc(L.soft_dve, 1)

                def subtract_maxima(k):
                    dve.wait_ge(L.soft_pe, k * 5 + 2)
                    dve.wait_ge(L.soft_dve, k * 6 + 2)
                    step(v.tensor_copy(cd[:, :], CD))
                    step(v.scalar_tensor_tensor(seg[:, :], penF[:, :], cd[:, 0:1], seg[:, :], ALU.add, ALU.max))
                    step(v.scalar_tensor_tensor(seg[:, :], penL[:, :], cd[:, 1:2], seg[:, :], ALU.add, ALU.max))
                    step(v.tensor_tensor(ecar[0:1, 0:1], rowC[0:1, 0:1], seg[0:1, 0:1], ALU.subtract))
                    v.tensor_tensor(seg[:, :], score_sb[:, :], seg[:, :], ALU.subtract).then_inc(L.soft_dve, 1)

                def row_sums(k):
                    dve.wait_ge(L.soft_act, k + 1)
                    v.tensor_tensor_scan(scanF[:, :], keep[:, 0:P], aexp[:, :], 0.0, ALU.mult, ALU.add)
                    step(v.tensor_tensor_scan(scanB[:, ::-1], keep[:, P:0:-1], aexp[:, ::-1], 0.0, ALU.mult, ALU.add))
                    step(v.tensor_tensor(seg[:, :], scanF[:, :], aexp[:, :], ALU.subtract))
                    v.tensor_tensor(seg[:, :], seg[:, :], scanB[:, :], ALU.add).then_inc(L.soft_dve, 1)

                def normalise(k):
                    dve.wait_ge(L.soft_pe, k * 5 + 4)
                    dve.wait_ge(L.soft_dve, k * 6 + 5)
                    step(v.tensor_copy(cd[:, :], SCD))
                    step(v.scalar_tensor_tensor(seg[:, :], isF[:, :], cd[:, 0:1], seg[:, :], ALU.mult, ALU.add))
                    step(v.scalar_tensor_tensor(seg[:, :], isL[:, :], cd[:, 1:2], seg[:, :], ALU.mult, ALU.add))
                    step(v.reciprocal(cfac[0:1, 0:1], seg[0:1, 0:1]))
                    v.tensor_tensor(cfac[0:1, 0:1], sumC[0:1, 0:1], cfac[0:1, 0:1], ALU.mult
                                    ).then_inc(L.soft_dve, 1)

                def weight_cols(k):
                    above(dve, L.a_made, k * (GC // 2 if narrow else GC))
                    dve.wait_ge(L.soft_pe, k * 5 + 5)
                    v.tensor_copy(relc[:, :], rel_col[:, bass.ds(k * TC, TC)])
                    v.tensor_copy(wcol[:, TC:TC + 1], CCOL)
                    step(v.reciprocal(rcol[:, :], TCOL))
                    step(v.tensor_tensor(wcol[:, 0:TC], ACOL, rcol[:, :], ALU.mult))

                def rescale(base):
                    col = numT[:, bass.ds(base, 1)]
                    step(v.tensor_scalar(col, col, wcol[:, TC:TC + 1], None, ALU.mult))

                def weighted_onehot(k, g):
                    n, s = k * GC + g, g % 2
                    if narrow:
                        a, both = apair[g // 2 % 2], (P, 2 * TG, WIN)
                        of = lambda cols: cols[:, g * TG:(g + 2) * TG].unsqueeze(2).broadcast_to(both)
                        above(dve, L.num_made, n - 2)
                        step(v.tensor_tensor(a, iota_row[:, 0:WIN].unsqueeze(1).broadcast_to(both), of(relc),
                                             ALU.is_equal))
                        v.tensor_tensor(a, a, of(wcol), ALU.mult).then_inc(L.a_made, 1)
                        return
                    above(dve, L.num_made, n - 1)
                    for i in range(TG):
                        t = g * TG + i
                        last = v.tensor_scalar(amat[s][:, i, :], iota_row[:, :], relc[:, t:t + 1], wcol[:, t:t + 1],
                                               ALU.is_equal, ALU.mult)
                    last.then_inc(L.a_made, 1)

                def add_sums(n, g, node=None):
                    nodes = [node] if narrow else first_nodes(base_row, n * TG, TG)
                    dve.wait_ge(L.num_made, n + 1)
                    for i, node in enumerate(nodes):
                        w = WIN if narrow else P
                        win = numT[:, bass.ds(node, w)]
                        ins = v.tensor_tensor(win, win, bAG[g % 2][:, i * P:i * P + w], ALU.add)
                        if i < len(nodes) - 1:
                            step(ins)
                        else:
                            ins.then_inc(L.num_added, 1)
                            dve.wait_ge(L.num_added, n + 1)

                def first_nodes(row, at, count):
                    _, vals = nc.values_load_multi_w_load_instructions(
                        row[0:1, bass.ds(at, count)], engines=(DVE_,), min_val=0, max_val=N,
                        skip_runtime_bounds_check_because=SORTED)
                    return vals

                def one_hot(c, g):
                    n, s, q = c * GC + g, g % 2, g % GS
                    dve.wait_ge(L.loaded[q], (c * (GC // GS) + g // GS + 1) * ready)
                    above(dve, L.z_made, n - 1)
                    v.tensor_scalar(onehot[s][:, :], rel_bc[q][:, :], (iota_win if narrow else iota_col)[:, 0:1], None,
                                    ALU.is_equal).then_inc(L.onehot_made, 1)

                def turn(c, front, soft, agg):
                    early = isinstance(c, int) and c == 2
                    if agg:
                        if narrow:
                            nodes = ([None] * TG + list(first_nodes(group_row, 0, GC)) if early else
                                     first_nodes(group_row, c * GC - (2 * GC + TG), GC + TG))[TG - 1:]
                        else:
                            nodes = [None] + list(first_nodes(group_row, c * GC - 2 * GC, TG)) + [None] * GC
                    for g in range(GC):
                        n, s, q = c * GC + g, g % 2, g % GS
                        if front and not (isinstance(c, int) and n == NG - 1):
                            one_hot(c, g + 1)
                        if soft:
                            if g == 0:
                                masks(c - 1)
                            if g == 1:
                                row_maxima(c - 1)
                            if g == 2:
                                dve.wait_ge(L.soft_dve, (c - 1) * 6 + 1)
                                chain(c - 1, 2, END_F, END_B, None, rowC, rowD, penA, penE, penC,
                                      ALU.add, ALU.max, -BIG)
                            if g == 3:
                                subtract_maxima(c - 1)
                            if g == 4:
                                row_sums(c - 1)
                            if g == 5:
                                dve.wait_ge(L.soft_dve, (c - 1) * 6 + 4)
                                chain(c - 1, 4, SEND_F, SEND_B, ecar[0:1, 1:2], sumC, sumD, keepA, keepE, cont,
                                      ALU.mult, ALU.add, 0.0)
                            if g == 6:
                                normalise(c - 1)
                        if agg:
                            if not (early and g == 0):
                                add_sums((c - 2) * GC + g - 1, (g - 1) % 2, nodes[g])
                            if g == 0:
                                rescale(nodes[1])
                            if not narrow:
                                weighted_onehot(c - 2, g)
                            elif g % 2 == 1 and g < GC - 1:
                                weighted_onehot(c - 2, g + 1)
                        if soft and g == GC - 1:
                            weight_cols(c - 1)
                            if narrow:
                                weighted_onehot(c - 1, 0)
                        if front:
                            dve.wait_ge(L.z_copied, n + 1)
                            above(dve, L.score_made, n - 1)
                            v.scalar_tensor_tensor(fT[s][:, :], zc[s][:, :], SLOPE, zc[s][:, :], ALU.mult, ALU.max
                                                   ).then_inc(L.f_made, 1)
                            if one:
                                above(dve, L.h1_stored[q], (c * (GC // GS) + g // GS) * 16)
                                v.scalar_tensor_tensor(h1[q][:, :], zc[s][:, :], 0.0, edge_in[q][:, :],
                                                       ALU.max, ALU.add).then_inc(L.h1_made, 1)

                one_hot(0, 0)
                for c in range(3):
                    turn(c, True, c >= 1, c >= 2)
                start, step.k = step.k, 0
                with dve.Fori(0, CH - 4) as j:
                    step.base = j * STEPS[narrow] + start
                    turn(j + 3, True, True, True)
                assert step.k == STEPS[narrow], step.k
                step.base, step.k = 0, start + (CH - 4) * STEPS[narrow]
                turn(CH - 1, True, True, True)
                turn(CH, False, True, True)
                turn(CH + 1, False, False, True)
                add_sums(NG - 1, 1, first_nodes(group_row, NG - TG, TG)[TG - 1])

            def either(L):
                with dve.If(fit == 1):
                    layer(L, True)
                with dve.Else():
                    layer(L, False)

            either(L1)

            def middle(m, s, q, t):
                if not isinstance(m, int) or m < NS:
                    dve.wait_ge(m_in[q], (t + 1) * 16)
                    dve.wait_ge(m_ht, m + 1)
                    above(dve, m_rows, m - 1)
                    v.scalar_tensor_tensor(zs[s][:, :], bZ[s][:, :], 0.0, slab[q], ALU.max, ALU.add
                                           ).then_inc(m_h0, 1)
                dve_parts(dve, m_parts, m, q, t, 1)

            slabs(dve, middle)
            for m in (NS, NS + 1):
                middle(m, m % 2, m % 4, m // 4)
            v.memset(numT[:, :], 0.0).then_inc(m_zero, 1)
            dve.wait_ge(m_zero, 1)
            either(L2)

            order = Steps(dve, e_dve)

            def y_sum(m, s, q, t):
                dve.wait_ge(e_in[q], (t + 1) * 16)
                dve.wait_ge(e_ht, m + 1)
                above(dve, e_rows, m - 1)
                v.scalar_tensor_tensor(zs[s][:, :], slab[q], 2.0, bZ[s][:, :], ALU.mult, ALU.add
                                       ).then_inc(e_y, 1)

            def moments(m, s):
                order.base, order.k = m * END_STEPS, 0
                dve.wait_ge(e_rows, m + 1)
                for b in range(TG):
                    last = v.bn_stats(stats[:, b, :], bAG[s][:, b * P:b * P + P])
                order(last)
                dve.sem_inc(dve_passed, 1)
                for b in range(TG):
                    last = v.bn_aggr(mv[:, b, :], stats[:, b, :])
                order(last)
                v.tensor_scalar(std[:, :], mv[:, :, 1], EPS, None, ALU.add).then_inc(e_var, 1)
                above(dve, e_out, m)
                dve.wait_ge(e_std, m + 1)
                order(v.reciprocal(rstd[:, :], std[:, :]))
                v.scalar_tensor_tensor(shift[:, :], mv[:, :, 0], -1.0, rstd[:, :], ALU.mult, ALU.mult
                                       ).then_inc(e_norm, 1)

            def end(m, s, q, t):
                y_sum(m, s, q, t)
                if not isinstance(m, int) or m >= 1:
                    moments(m - 1, 1 - s)

            slabs(dve, end)
            moments(NS - 1, (NS - 1) % 2)


END_STEPS = 3
STEPS = {True: 22, False: 42}


def kernel(**inputs):
    import numpy as np
    import concourse.bacc as bacc
    from concourse import mybir as _mybir
    from concourse.bass_utils import run_bass_kernel_spmd as run

    x = np.asarray(inputs["x"])
    src = np.asarray(inputs["src"])
    dst = np.asarray(inputs["dst"])
    edges = np.asarray(inputs["edge_attr_128"])
    ep = NT * P
    srcp = np.concatenate([src, np.zeros(ep - E, src.dtype)])
    dstp = np.concatenate([dst, np.full(ep - E, N, dst.dtype)])
    edgep = np.concatenate([edges, np.zeros((ep - E, D), edges.dtype)])
    xp = np.concatenate([x, np.zeros((NP - N, D), x.dtype)])
    t = np.ascontiguousarray
    arrays = {
        "eT": t(edgep.reshape(NG, W, D).transpose(0, 2, 1)),
        "xT": t(xp.T),
        "xrows": t(x),
        "idxT": t(srcp.reshape(NT, P).T),
        "dstT": t(dstp.reshape(NT, P).T),
        "dstR": t(dstp.reshape(CH, TC, P).transpose(1, 0, 2)),
        "dst8": t(dstp.reshape(NT // 8, 8, P)),
        "ends": t(dstp.reshape(NT, P)[:, [0, P - 1]].T),
    }
    for layer in ("1", "2"):
        for w in ("fij", "ni", "nj", "node"):
            arrays[f"w_{w}{layer}"] = t(np.asarray(inputs[f"L0_gnn_W{layer}_{w}"]).T)
        arrays[f"attn{layer}"] = t(np.asarray(inputs[f"L0_gnn_attn{layer}"]).reshape(D, 1))
    nc = bacc.Bacc("TRN2", target_bir_lowering=False, num_devices=1)
    args = {n: nc.dram_tensor(n, a.shape, _mybir.dt.from_np(a.dtype), kind="ExternalInput").ap()
            for n, a in arrays.items()}
    out = nc.dram_tensor("out", (N, D), _mybir.dt.from_np(x.dtype), kind="ExternalOutput").ap()
    program(nc, out=out, **args)
    r = run(nc, [arrays], core_ids=[0])
    return r.results[0]["out"]
```
